# Optimizing a Trainium2 kernel written in Bass

```python
import numpy as np
import jax
import jax.numpy as jnp

def _softmax(x, axis=-1):
    return jax.nn.softmax(x, axis=axis)

def _gelu(x):
    return jax.nn.gelu(x, approximate=True)

def _silu(x):
    return jax.nn.silu(x)

def _sigmoid(x):
    return jax.nn.sigmoid(x)

def _layernorm(x, axis=-1, eps=1e-05):
    m = jnp.mean(x, axis=axis, keepdims=True)
    v = jnp.var(x, axis=axis, keepdims=True)
    return (x - m) / jnp.sqrt(v + eps)

def _scatter_add(tgt, idx, src, axis=0):
    return tgt.at[idx].add(src)

def _segment_sum(src, seg, n):
    return jax.ops.segment_sum(src, seg, n)
kernel_name = 'mk_macaron_d1_jaxref_r8_c68d62'

def setup_inputs(seed: int=0):
    np.random.seed(seed)
    _w = jnp.asarray

    def _L0_attn_setup():
        import jax, jax.numpy as jnp
        import numpy as np
        SHIFTS = (-32, -16, -4, -1, 1, 4, 16, 32)
        LN_EPS = 1e-05
        key = jax.random.key(seed)
        k_x, k_g, k_v, k_gm, k_bt = jax.random.split(key, 5)
        B, L, D = (4, 512, 128)
        n = len(SHIFTS) + 1
        scale = 1.0 / np.sqrt(D)
        x = jax.random.normal(k_x, (B, L, D), dtype=jnp.float32)
        gate_W = jax.random.normal(k_g, (n * D, D), dtype=jnp.float32) * scale
        value_W = jax.random.normal(k_v, (D, D), dtype=jnp.float32) * scale
        gamma = jnp.ones((D,), dtype=jnp.float32)
        beta = jnp.zeros((D,), dtype=jnp.float32)
        return {'x': x, 'gate_W': gate_W, 'value_W': value_W, 'gamma': gamma, 'beta': beta}
    _L0_attn_in = _L0_attn_setup()

    def _L0_ffn_setup():
        import jax, jax.numpy as jnp
        import numpy as np
        HIDDEN = 128
        NUM_EXPERTS = 8
        TOP_K = 2
        key = jax.random.key(seed)
        k_x, k_r, k_w1, k_w2 = jax.random.split(key, 4)
        x = jax.random.normal(k_x, (4, 256, HIDDEN), dtype=jnp.float32)
        router_w = jax.random.normal(k_r, (NUM_EXPERTS, HIDDEN), dtype=jnp.float32) * HIDDEN ** (-0.5)
        w1 = jax.random.normal(k_w1, (NUM_EXPERTS, HIDDEN, 2 * HIDDEN), dtype=jnp.float32) * HIDDEN ** (-0.5)
        w2 = jax.random.normal(k_w2, (NUM_EXPERTS, 2 * HIDDEN, HIDDEN), dtype=jnp.float32) * (2 * HIDDEN) ** (-0.5)
        return {'x': x, 'router_w': router_w, 'w1': w1, 'w2': w2}
    _L0_ffn_in = _L0_ffn_setup()
    _d = {'L0_attn_x': _L0_attn_in['x'], 'L0_attn_gate_W': _L0_attn_in['gate_W'], 'L0_attn_value_W': _L0_attn_in['value_W'], 'L0_attn_gamma': _L0_attn_in['gamma'], 'L0_attn_beta': _L0_attn_in['beta'], 'L0_ffn_router_w': _L0_ffn_in['router_w'], 'L0_ffn_w1': _L0_ffn_in['w1'], 'L0_ffn_w2': _L0_ffn_in['w2']}
    _x0 = _d['L0_attn_x']
    _d['L0_attn_x'] = jax.random.normal(jax.random.fold_in(jax.random.key(seed), 1), (4, 1024, 128), dtype=_x0.dtype)
    del _x0
    return _d

def reference(L0_attn_x, L0_attn_gate_W, L0_attn_value_W, L0_attn_gamma, L0_attn_beta, L0_ffn_router_w, L0_ffn_w1, L0_ffn_w2):

    def _L0_attn_ref(x, gate_W, value_W, gamma, beta):
        import jax, jax.numpy as jnp
        import numpy as np
        SHIFTS = (-32, -16, -4, -1, 1, 4, 16, 32)
        LN_EPS = 1e-05
        B, L, D = x.shape
        n = len(SHIFTS) + 1
        v = jnp.einsum('bld,ed->ble', x, value_W)
        stacked = jnp.stack([v] + [jnp.roll(v, -s, axis=1) for s in SHIFTS], axis=2)
        gates = jax.nn.sigmoid(jnp.einsum('bld,ed->ble', x, gate_W))
        gates = gates.reshape(B, L, n, D)
        out = jnp.sum(stacked * gates, axis=2)
        mu = jnp.mean(out, axis=-1, keepdims=True)
        var = jnp.mean(jnp.square(out - mu), axis=-1, keepdims=True)
        return (out - mu) * jax.lax.rsqrt(var + LN_EPS) * gamma + beta

    def _L0_ffn_ref(x, router_w, w1, w2):
        import jax, jax.numpy as jnp
        import numpy as np
        HIDDEN = 128
        NUM_EXPERTS = 8
        TOP_K = 2
        bsz, seq, hidden = x.shape
        tokens = x.reshape(-1, hidden)
        logits = tokens @ router_w.T
        topk_vals, topk_idx = jax.lax.top_k(logits, TOP_K)
        weights = jax.nn.softmax(topk_vals, axis=-1)
        h = jnp.einsum('td,edf->etf', tokens, w1)
        h = jax.nn.gelu(h, approximate=False)
        out_all = jnp.einsum('etf,efd->etd', h, w2)
        out_ted = jnp.transpose(out_all, (1, 0, 2))
        gathered = jnp.take_along_axis(out_ted, topk_idx[:, :, None], axis=1)
        output = jnp.sum(weights[:, :, None] * gathered, axis=1)
        return output.reshape(bsz, seq, hidden)
    x = L0_attn_x
    x = x + 0.5 * _L0_ffn_ref(_layernorm(x, axis=-1), L0_ffn_router_w, L0_ffn_w1, L0_ffn_w2)
    x = x + _L0_attn_ref(_layernorm(x, axis=-1), L0_attn_gate_W, L0_attn_value_W, L0_attn_gamma, L0_attn_beta)
    x = x + 0.5 * _L0_ffn_ref(_layernorm(x, axis=-1), L0_ffn_router_w, L0_ffn_w1, L0_ffn_w2)
    return x

_drawn_inputs = setup_inputs


def setup_inputs(seed=0):
    import zlib

    import numpy as np

    out = dict(_drawn_inputs(seed))
    spreads = {'L0_attn_gamma': (1.0, 0.2), 'L0_attn_beta': (0.0, 0.1)}
    factors = {}
    for name, (base, spread) in spreads.items():
        noise = np.random.default_rng([zlib.crc32(name.encode()), seed]).standard_normal(out[name].shape)
        drawn = base * np.exp(spread * noise) if base else spread * noise
        out[name] = jnp.asarray(drawn.astype(out[name].dtype))
    for name, factor in factors.items():
        out[name] = (out[name] * factor).astype(out[name].dtype)
    return out
```

```python
from contextlib import ExitStack

import concourse.bass as bass
from concourse import mybir

F32 = mybir.dt.float32
F32R = mybir.dt.float32r
ALU = mybir.AluOpType
ACT = mybir.ActivationFunctionType
AX_X = mybir.AxisListType.X

P = 128
SHIFTS = (0, -32, -16, -4, -1, 1, 4, 16, 32)
LN_EPS = 1e-05
BELOW_ALL = -3.0e38


def macaron_program(nc, x_in, gate_W, value_W, gamma, beta, router_w, w1, w2, out):
    BATCH, SEQ, D = x_in.shape
    E, _, FF = w1.shape
    T = BATCH * SEQ
    BLK = 512
    TPB = BLK // P
    NB = T // BLK
    BPS = SEQ // BLK
    FH = FF // P
    NS = len(SHIFTS)
    U = NS + 1
    HALO = max(SHIFTS)
    LAG = 3
    HB = 4
    TPS = SEQ // P
    assert D == P and FH == 2 and BPS == 2 and E % HB == 0 and LAG < HB and E == 8
    POOL_UNITS = (2, 5, 8)
    DVE_UNITS = tuple(u for u in range(1, U) if u not in POOL_UNITS)
    NPU, NDU = len(POOL_UNITS), len(DVE_UNITS)

    x_tiles = x_in.rearrange("b s d -> (b s) d").rearrange("(n p) d -> p n d", p=P)
    out_tiles = out.rearrange("b s d -> (b s) d").rearrange("(n p) d -> p n d", p=P)

    def zero(n):
        return isinstance(n, int) and n == 0

    with ExitStack() as ctx:
        def sb(name, shape, dt=F32):
            return ctx.enter_context(nc.sbuf_tensor(name, shape, dt))

        def psum(name, shape):
            return ctx.enter_context(nc.psum_tensor(name, shape, F32))

        def sem(name):
            return ctx.enter_context(nc.semaphore(name))

        x_res = sb("x_res", [P, NB * TPB, D])
        xT_hi = sb("xT_hi", [P, NB, BLK], F32R)
        xT_lo = sb("xT_lo", [P, NB, BLK], F32R)
        w1_hi = sb("w1_hi", [P, E, FF], F32R)
        w1_lo = sb("w1_lo", [P, E, FF], F32R)
        w2_hi = sb("w2_hi", [P, E, FH, D], F32R)
        w2_lo = sb("w2_lo", [P, E, FH, D], F32R)
        mix_hi = sb("mix_hi", [P, U, P], F32R)
        mix_lo = sb("mix_lo", [P, U, P], F32R)
        rt_hi = sb("rt_hi", [P, E], F32R)
        rt_lo = sb("rt_lo", [P, E], F32R)
        gelu_h = sb("gelu_h", [P, 2, FH, BLK])
        scaled_h = sb("scaled_h", [P, HB, FH, BLK])
        h_hi = sb("h_hi", [P, HB, FH, BLK], F32R)
        h_lo = sb("h_lo", [P, HB, FH, BLK], F32R)
        pool_mix = sb("pool_mix", [P, 2, SEQ])
        v_pad = sb("v_pad", [P, 2, SEQ + 2 * HALO])
        mixed = sb("mixed", [P, SEQ])
        z_mix = sb("z_mix", [P, TPS, D])
        xn_ffn = sb("xn_ffn", [P, TPB, D])
        xn_mix = sb("xn_mix", [P, TPB, D])
        yT = sb("yT", [P, BLK])
        lgT = sb("lgT", [P, BLK])
        wT = sb("wT", [P, 2, BLK], F32R)
        sel = sb("sel", [P, E, P], F32R)
        sel_raw = sb("sel_raw", [P, E, P])
        rt_raw = sb("rt_raw", [E, D])
        ident = sb("ident", [P, P])
        gamma_b = sb("gamma_b", [P, D])
        beta_b = sb("beta_b", [P, D])
        stats = sb("stats", [P, 2, TPB, 6])
        mv = sb("mv", [P, 2, TPB, 2])
        veps = sb("veps", [P, 2, TPB])
        rstd = sb("rstd", [P, 2, TPB])
        stats_o = sb("stats_o", [P, TPS, 6])
        mv_o = sb("mv_o", [P, TPS, 2])
        veps_o = sb("veps_o", [P, TPS])
        rstd_o = sb("rstd_o", [P, TPS])
        nbias_o = sb("nbias_o", [P, TPS])
        m_half = sb("m_half", [P, TPS])
        eps_c = sb("eps_c", [P, TPS])
        wait_pad = sb("wait_pad", [P, 1])
        rank = sb("rank", [P, TPB, E])
        top = sb("top", [P, 8, TPB])
        pick = sb("pick", [P, 6, TPB, E])
        w16 = sb("w16", [P, TPB, 2 * E])

        ps_up = psum("ps_up", [P, 2, FH, BLK])
        ps_out = psum("ps_out", [P, 2, BLK])
        ps_t = psum("ps_t", [P, TPB, P])
        ps_r = psum("ps_r", [P, BLK])
        ps_y, ps_w = ps_out[:, 0, :], ps_out[:, 1, :]
        logits = ps_r[:, :].rearrange("p (t c) -> p t c", c=P)[:, :, 0:E]

        w1_raw = scaled_h[:, 0:2, :, :].rearrange("p a k c -> p (a k c)").rearrange("p (e f) -> p e f", e=E)
        w2_raw = scaled_h[:, 2:4, :, :].rearrange("p a k c -> p (a k c)").rearrange("p (e k d) -> p e k d", e=E, k=FH)
        mix_raw = pool_mix[:, :, :].rearrange("p a c -> p (a c)")[:, 0:U * D].rearrange("p (u d) -> p u d", u=U)
        acc_d, prod_d = gelu_h[:, 0, :, :].rearrange("p k c -> p (k c)"), gelu_h[:, 1, :, :].rearrange("p k c -> p (k c)")
        acc_p, prod_p = pool_mix[:, 0, :], pool_mix[:, 1, :]

        s_x0, s_x1, s_w1, s_w2, s_rt, s_mixw, s_gb = (sem(n) for n in ("x0_in", "x1_in", "w1_in", "w2_in", "rt_in", "mixw_in", "gb_in"))
        s_zero, s_const = sem("consts_cleared"), sem("consts_ready")
        s_sel, s_rank, s_pad = sem("sel_ready"), sem("rank_ready"), sem("rows_cleared")
        s_rtT, s_rts = sem("router_turned"), sem("router_split")
        s_w1h, s_w1l, s_w2h, s_w2l = (sem(n) for n in ("w1_hi_ready", "w1_lo_ready", "w2_hi_ready", "w2_lo_ready"))
        s_mixT, s_mixh, s_mixl = sem("mixw_turned"), sem("mixw_hi_ready"), sem("mixw_lo_ready")

        class Norm:
            def __init__(self, n):
                self.link, self.stat, self.veps, self.rstd, self.xn, self.turned, self.split = (
                    sem(f"{n}_{k}") for k in ("link", "stats_ready", "veps_ready", "rstd_ready", "xn_ready", "turned", "split"))
        nf, nm = Norm("ffn"), Norm("mix")
        s_lg, s_lgT, s_lgt = sem("logitsT_ready"), sem("logitsT_copied"), sem("logits_ready")
        s_tl, s_gap, s_tanh, s_w16, s_wt, s_wT = (sem(n) for n in ("top_link", "gap_ready", "tanh_ready", "w16_ready", "wT_turned", "wT_ready"))
        s_up, s_bc, s_gelu, s_scaled, s_hi, s_lo, s_down = (
            sem(n) for n in ("up_done", "weights_spread", "gelu_done", "scaled_done", "h_hi_done", "h_lo_done", "down_done"))
        s_yT, s_yt, s_xnew = sem("yT_copied"), sem("y_turned"), sem("x_updated")
        s_mm, s_v, s_gate, s_dg, s_pg, s_dl, s_pl = (
            sem(n) for n in ("mix_product_done", "value_copied", "gate_ready", "dve_gate_used", "pool_gate_used", "dve_mix_link", "pool_mix_link"))
        s_psum_p, s_mixed, s_ot, s_ol, s_ostat, s_oveps, s_orstd, s_nb, s_z, s_zg, s_xb, s_xmix = (
            sem(n) for n in ("pool_sum_ready", "mixed_ready", "mixed_turned", "out_link", "out_stats_ready", "out_veps_ready",
                             "out_rstd_ready", "out_bias_ready", "z_ready", "z_gamma_ready", "x_beta_ready", "x_mixed"))
        s_out = sem("out_stored")

        def xblk(b):
            return x_res[:, bass.ds(b * TPB, TPB), :]

        block = ctx.enter_context(nc.Block())

        @block.sync
        def _(sp):
            sp.dma_start(x_res[:, 0:TPB, :], x_tiles[:, 0:TPB, :]).then_inc(s_x0, 16)
            sp.dma_start(w1_raw, w1.rearrange("e d f -> d e f")).then_inc(s_w1, 16)
            sp.dma_start(rt_raw[:], router_w).then_inc(s_rt, 16)
            sp.dma_start(w2_raw, w2.rearrange("e (k p) d -> p e k d", p=P)).then_inc(s_w2, 16)
            sp.dma_start(mix_raw[:, 0:1, :], value_W.rearrange("(u e) d -> e u d", e=P)).then_inc(s_mixw, 16)
            sp.dma_start(mix_raw[:, 1:U, :], gate_W.rearrange("(u e) d -> e u d", e=P)).then_inc(s_mixw, 16)
            sp.dma_start(x_res[:, TPB:, :], x_tiles[:, TPB:, :]).then_inc(s_x1, 16)
            sp.dma_start(gamma_b[:], gamma.rearrange("(a d) -> a d", a=1).partition_broadcast(P)).then_inc(s_gb, 16)
            sp.dma_start(beta_b[:], beta.rearrange("(a d) -> a d", a=1).partition_broadcast(P)).then_inc(s_gb, 16)
            with sp.Fori(0, NB) as b:
                sp.wait_ge(s_xnew, b + NB + 1)
                sp.dma_start(out_tiles[:, bass.ds(b * TPB, TPB), :], xblk(b)).then_inc(s_out, 16)
            sp.wait_ge(s_out, 16 * NB)

        @block.tensor
        def _(pe):
            def turn_x(s, xn, n, free):
                pe.wait_ge(s.xn, n + 1)
                for sm, v in free:
                    pe.wait_ge(sm, v)
                for j in range(TPB):
                    t = pe.transpose(ps_t[:, j, :], xn[:, j, :], ident[:])
                t.then_inc(s.turned, 1)

            def router(b, n):
                pe.wait_ge(nf.split, 2 * n + 2)
                if not zero(n):
                    pe.wait_ge(s_wT, n)
                pe.matmul(ps_r[0:E, :], rt_hi[:], xT_hi[:, bass.ds(b, 1), :], start=True, stop=False)
                pe.matmul(ps_r[0:E, :], rt_hi[:], xT_lo[:, bass.ds(b, 1), :], start=False, stop=False)
                pe.matmul(ps_r[0:E, :], rt_lo[:], xT_hi[:, bass.ds(b, 1), :], start=False, stop=True).then_inc(s_lg, 1)

            def turn_logits(n):
                pe.wait_ge(s_lgT, n + 1)
                for j in range(TPB):
                    t = pe.transpose(ps_r[:, j * P:(j + 1) * P], lgT[:, j * P:(j + 1) * P], ident[:])
                t.then_inc(s_lgt, 1)

            def turn_weights(n):
                pe.wait_ge(s_w16, n + 1)
                for j in range(TPB):
                    t = pe.transpose(ps_r[0:2 * E, j * P:(j + 1) * P], w16[:, j, :], ident[:])
                t.then_inc(s_wt, 1)

            def up(b, e, g, warm):
                if warm:
                    pe.wait_ge(s_gelu, g - 1)
                for k in range(FH):
                    w = slice(k * P, (k + 1) * P)
                    pe.matmul(ps_up[:, e % 2, k, :], w1_hi[:, e, w], xT_hi[:, bass.ds(b, 1), :], start=True, stop=False)
                    pe.matmul(ps_up[:, e % 2, k, :], w1_hi[:, e, w], xT_lo[:, bass.ds(b, 1), :], start=False, stop=False)
                    t = pe.matmul(ps_up[:, e % 2, k, :], w1_lo[:, e, w], xT_hi[:, bass.ds(b, 1), :], start=False, stop=True)
                t.then_inc(s_up, 1)

            def spread(e, g, n, par):
                if e == 0:
                    pe.wait_ge(s_wT, n + 1)
                if not zero(g):
                    pe.wait_ge(s_scaled, g)
                pe.matmul(ps_w, sel[:, e, :], wT[:, bass.ds(par, 1), :], start=True, stop=True).then_inc(s_bc, 1)

            def down(e, g, n):
                pe.wait_ge(s_hi, g + 1)
                pe.wait_ge(s_lo, g + 1)
                if e == 0 and not zero(n):
                    pe.wait_ge(s_yT, n)
                for k in range(FH):
                    pe.matmul(ps_y, w2_hi[:, e, k, :], h_hi[:, e % HB, k, :], start=(e == 0 and k == 0), stop=False)
                    pe.matmul(ps_y, w2_lo[:, e, k, :], h_hi[:, e % HB, k, :], start=False, stop=False)
                    t = pe.matmul(ps_y, w2_hi[:, e, k, :], h_lo[:, e % HB, k, :], start=False, stop=(e == E - 1 and k == FH - 1))
                t.then_inc(s_down, 1)

            def turn_y(n, free):
                pe.wait_ge(s_yT, n + 1)
                for sm, v in free:
                    pe.wait_ge(sm, v)
                for j in range(TPB):
                    t = pe.transpose(ps_t[:, j, :], yT[:, j * P:(j + 1) * P], ident[:])
                t.then_inc(s_yt, 1)

            def ffn_block(layer, b, first, last, second=False):
                n = layer * NB + b
                cold = first and layer == 0
                for e in range(E):
                    g = n * E + e
                    if first and e == 0:
                        pe.wait_ge(nf.split, 2 * n + 2)
                    up(b, e, g, not (cold and e < 2))
                    spread(e, g, n, b % 2)
                    if e >= LAG:
                        down(e - LAG, g - LAG, n)
                    elif not first:
                        down(e - LAG + E, g - LAG, n - 1)
                    if e == 2 and not last:
                        if first or second:
                            free = []
                        else:
                            free = [(nm.split, 2 * b - 2)] if layer == 0 else [(s_xnew, n - 1)]
                        turn_x(nf, xn_ffn, n + 1, free)
                    if e == 3 and not last:
                        router(b + 1, n + 1)
                    if e == 4 and not first:
                        if not last:
                            free = [(nf.split, 2 * n + 4)]
                        else:
                            free = [(nm.split, 2 * b - 2)] if layer == 0 else [(s_xnew, n - 1)]
                        turn_y(n - 1, free)
                    if e == 5 and not last:
                        turn_logits(n + 1)
                    if e == 7:
                        if not last:
                            turn_weights(n + 1)
                        if layer == 0 and not first:
                            turn_x(nm, xn_mix, b - 1, [(s_xnew, b)])

            def ffn_layer(layer):
                ffn_block(layer, 0, True, False)
                if layer == 0:
                    ffn_block(layer, 1, False, False, second=True)
                with pe.Fori(2 - layer, NB - 1) as b:
                    ffn_block(layer, b, False, False)
                ffn_block(layer, NB - 1, False, True)
                n = layer * NB + NB - 1
                for e in range(E - LAG, E):
                    down(e, n * E + e, n)
                turn_y(n, [(nm.split, 2 * NB - 2)] if layer == 0 else [(s_xnew, n)])
                if layer == 0:
                    turn_x(nm, xn_mix, NB - 1, [(s_xnew, NB)])

            def turn_mixed(i):
                pe.wait_ge(s_mixed, i + 1)
                if not zero(i):
                    pe.wait_ge(s_z, i)
                for j in range(TPS):
                    t = pe.transpose(ps_out[:, j // TPB, (j % TPB) * P:(j % TPB + 1) * P], mixed[:, j * P:(j + 1) * P], ident[:])
                t.then_inc(s_ot, 1)

            def mix_seq(i, first):
                for u in range(U):
                    q = i * U + u
                    if not (first and u < 2):
                        if u == 0:
                            pe.wait_ge(s_gate, i * NS - 1)
                        elif u == 1:
                            pe.wait_ge(s_gate, i * NS)
                        elif u == 2:
                            pe.wait_ge(s_v, i + 1)
                        else:
                            pe.wait_ge(s_gate, i * NS + u - 2)
                    for k in range(BPS):
                        if u == 0:
                            pe.wait_ge(nm.split, 4 * i + 2 * k + 2)
                        xb = bass.ds(i * BPS + k, 1)
                        pe.matmul(ps_up[:, u % 2, k, :], mix_hi[:, u, :], xT_hi[:, xb, :], start=True, stop=False)
                        pe.matmul(ps_up[:, u % 2, k, :], mix_hi[:, u, :], xT_lo[:, xb, :], start=False, stop=False)
                        t = pe.matmul(ps_up[:, u % 2, k, :], mix_lo[:, u, :], xT_hi[:, xb, :], start=False, stop=True)
                    t.then_inc(s_mm, 1)
                    if u == 3 and not first:
                        turn_mixed(i - 1)

            pe.wait_ge(s_const, 1)
            pe.wait_ge(s_rt, 16)
            pe.transpose(ps_t[:, 0, 0:E], rt_raw[:], ident[0:E, 0:E]).then_inc(s_rtT, 1)
            turn_x(nf, xn_ffn, 0, [(s_rts, 2)])
            pe.wait_ge(s_mixw, 32)
            for u in range(8):
                t = pe.transpose(ps_out[:, u // TPB, (u % TPB) * P:(u % TPB + 1) * P], mix_raw[:, u, :], ident[:])
            t.then_inc(s_mixT, 1)
            router(0, 0)
            turn_logits(0)
            pe.wait_ge(s_mixl, 1)
            for u in range(8, U):
                t = pe.transpose(ps_out[:, 0, (u - 8) * P:(u - 7) * P], mix_raw[:, u, :], ident[:])
            t.then_inc(s_mixT, 1)
            turn_weights(0)
            pe.wait_ge(s_w1h, 1)
            pe.wait_ge(s_w1l, 1)
            pe.wait_ge(s_w2h, 1)
            pe.wait_ge(s_w2l, 1)
            pe.wait_ge(s_sel, 1)
            pe.wait_ge(s_mixl, 2)
            ffn_layer(0)
            mix_seq(0, True)
            with pe.Fori(1, BATCH) as i:
                mix_seq(i, False)
            turn_mixed(BATCH - 1)
            turn_x(nf, xn_ffn, NB, [(nm.split, 2 * NB)])
            router(0, NB)
            turn_logits(NB)
            turn_weights(NB)
            pe.wait_ge(s_z, BATCH)
            ffn_layer(1)

        @block.scalar
        def _(act):
            def logits_copy(n):
                if zero(n):
                    act.wait_ge(s_pad, 2)
                act.wait_ge(s_lg, n + 1)
                act.activation(lgT[0:E, :], ps_r[0:E, :], ACT.Copy).then_inc(s_lgT, 1)

            def gap_tanh(n):
                act.wait_ge(s_gap, n + 1)
                act.activation(top[:, 5, :], top[:, 4, :], ACT.Tanh, scale=0.5).then_inc(s_tanh, 1)

            def gelu(e, g, warm):
                act.wait_ge(s_up, g + 1)
                if warm:
                    act.wait_ge(s_scaled, g - 1)
                act.activation(gelu_h[:, e % 2, :, :], ps_up[:, e % 2, :, :], ACT.Gelu).then_inc(s_gelu, 1)

            def h_round(e, g, warm):
                act.wait_ge(s_scaled, g + 1)
                if warm:
                    act.wait_ge(s_down, g - HB + 1)
                act.activation(h_hi[:, e % HB, :, :], scaled_h[:, e % HB, :, :], ACT.Copy).then_inc(s_hi, 1)

            def y_copy(n):
                act.wait_ge(s_down, (n + 1) * E)
                if not zero(n):
                    act.wait_ge(s_yt, n)
                act.activation(yT[:], ps_y, ACT.Copy).then_inc(s_yT, 1)

            def ffn_block(layer, b, first, last):
                n = layer * NB + b
                cold = first and layer == 0
                for e in range(E):
                    g = n * E + e
                    if e == LAG and not first:
                        y_copy(n - 1)
                    gelu(e, g, not (cold and e < 2))
                    if e >= 1:
                        h_round(e - 1, g - 1, not (cold and e - 1 < HB))
                    elif not first:
                        h_round(E - 1, g - 1, True)
                    if e == 4 and not last:
                        logits_copy(n + 1)
                    if e == 6 and not last:
                        gap_tanh(n + 1)

            def ffn_layer(layer):
                ffn_block(layer, 0, True, False)
                with act.Fori(1, NB - 1) as b:
                    ffn_block(layer, b, False, False)
                ffn_block(layer, NB - 1, False, True)
                n = layer * NB + NB - 1
                h_round(E - 1, n * E + E - 1, True)
                y_copy(n)

            def normalise_out(i):
                act.wait_ge(s_nb, i + 1)
                act.wait_ge(s_ot, i + 1)
                if not zero(i):
                    act.wait_ge(s_xmix, i)
                for j in range(TPS):
                    t = act.activation(z_mix[:, j, :], ps_out[:, j // TPB, (j % TPB) * P:(j % TPB + 1) * P], ACT.Identity,
                                       bias=nbias_o[:, j:j + 1], scale=rstd_o[:, j:j + 1])
                t.then_inc(s_z, 1)

            def gate(i, u, first):
                act.wait_ge(s_mm, i * U + u + 1)
                prev, turn = (u - HB, 0) if u > HB else ({1: 9, 2: 6, 3: 7, 4: 8}[u], 1)
                if not (first and turn):
                    if prev in POOL_UNITS:
                        act.wait_ge(s_pg, (i - turn) * NPU + POOL_UNITS.index(prev) + 1)
                    else:
                        act.wait_ge(s_dg, (i - turn) * NDU + DVE_UNITS.index(prev) + 1)
                act.activation(scaled_h[:, (u - 1) % HB, :, :], ps_up[:, u % 2, :, :], ACT.Sigmoid).then_inc(s_gate, 1)

            def value_copy(i, first):
                act.wait_ge(s_mm, i * U + 1)
                v = v_pad[:, bass.ds(i % 2, 1), :].rearrange("p a c -> p (a c)")
                pv = ps_up[:, 0, :, :].rearrange("p k c -> p (k c)")
                act.activation(v[:, HALO:HALO + SEQ], pv, ACT.Copy)
                act.activation(v[:, 0:HALO], pv[:, SEQ - HALO:SEQ], ACT.Copy)
                act.activation(v[:, HALO + SEQ:], pv[:, 0:HALO], ACT.Copy).then_inc(s_v, 1)

            def mix_seq(i, first):
                value_copy(i, first)
                for u in range(1, U):
                    gate(i, u, first)
                    if u == 5 and not first:
                        normalise_out(i - 1)

            act.wait_ge(s_w1, 16)
            act.activation(w1_hi[:], w1_raw, ACT.Copy).then_inc(s_w1h, 1)
            act.wait_ge(s_w2, 16)
            act.activation(w2_hi[:], w2_raw, ACT.Copy).then_inc(s_w2h, 1)
            act.wait_ge(s_mixT, 1)
            act.activation(mix_hi[:, 0:8, :], ps_out[:, :, :], ACT.Copy).then_inc(s_mixh, 1)
            logits_copy(0)
            act.wait_ge(s_mixT, 2)
            act.activation(mix_hi[:, 8:U, :], ps_out[:, 0, 0:(U - 8) * P], ACT.Copy).then_inc(s_mixh, 1)
            gap_tanh(0)
            act.wait_ge(s_w1l, 1)
            act.wait_ge(s_w2l, 1)
            ffn_layer(0)
            act.wait_ge(s_lo, NB * E)
            mix_seq(0, True)
            with act.Fori(1, BATCH) as i:
                mix_seq(i, False)
            normalise_out(BATCH - 1)
            logits_copy(NB)
            gap_tanh(NB)
            ffn_layer(1)

        @block.vector
        def _(dve):
            def norm_stats(s, w, xb, n):
                for j in range(TPB):
                    t = dve.bn_stats(stats[:, w, j, :], xb(j))
                t.then_inc(s.link, 1)
                dve.wait_ge(s.link, n + 1)
                dve.memset(wait_pad[:], 0.0)
                for j in range(TPB):
                    t = dve.bn_aggr(mv[:, w, j, :], stats[:, w, j, :])
                t.then_inc(s.stat, 1)

            def norm_apply(s, w, xb, xn, n):
                dve.wait_ge(s.rstd, n + 1)
                for j in range(TPB):
                    t = dve.tensor_scalar(xn[:, j, :], xb(j), mv[:, w, j, 0:1], rstd[:, w, j:j + 1], ALU.subtract, ALU.mult)
                t.then_inc(s.xn, 1)

            def norm_split(s, b, n):
                dve.wait_ge(s.turned, n + 1)
                src = ps_t[:, :, :].rearrange("p j c -> p (j c)")
                hi = xT_hi[:, bass.ds(b, 1), :].rearrange("p a c -> p (a c)")
                lo = xT_lo[:, bass.ds(b, 1), :].rearrange("p a c -> p (a c)")
                dve.tensor_copy(hi, src).then_inc(s.split, 1)
                dve.wait_ge(s.split, 2 * n + 1)
                dve.tensor_tensor(lo, src, hi.bitcast(F32), ALU.subtract).then_inc(s.split, 1)

            TOP_LINKS = 17

            def link(t, n, k):
                t.then_inc(s_tl, 1)
                dve.wait_ge(s_tl, TOP_LINKS * n + k)

            def spread_e(ap):
                return ap.unsqueeze(2).broadcast_to([P, TPB, E])

            def top2(n):
                v1, r1, v2, r2, gap = (top[:, k, :] for k in range(5))
                k1, s1, lg2, k2, s2 = (pick[:, k, :, :] for k in range(5))
                dve.wait_ge(s_lgt, n + 1)
                link(dve.tensor_reduce(v1, logits, AX_X, ALU.max), n, 1)
                link(dve.tensor_tensor(k1, logits, spread_e(v1), ALU.is_equal), n, 2)
                link(dve.tensor_tensor(k1, k1, rank[:], ALU.mult), n, 3)
                link(dve.tensor_reduce(r1, k1, AX_X, ALU.max), n, 4)
                link(dve.tensor_tensor(s1, k1, spread_e(r1), ALU.is_equal), n, 5)
                link(dve.scalar_tensor_tensor(lg2, s1, BELOW_ALL, logits, ALU.mult, ALU.add), n, 6)
                link(dve.tensor_reduce(v2, lg2, AX_X, ALU.max), n, 7)
                dve.tensor_tensor(gap, v1, v2, ALU.subtract).then_inc(s_gap, 1)
                link(dve.tensor_tensor(k2, lg2, spread_e(v2), ALU.is_equal), n, 8)
                link(dve.tensor_tensor(k2, k2, rank[:], ALU.mult), n, 9)
                link(dve.tensor_reduce(r2, k2, AX_X, ALU.max), n, 10)
                link(dve.tensor_tensor(s2, k2, spread_e(r2), ALU.is_equal), n, 11)

            def expert_weights(n):
                th, wa, wb = (top[:, k, :] for k in (5, 6, 7))
                s1, s2, wsum = pick[:, 1, :, :], pick[:, 4, :, :], pick[:, 5, :, :]
                dve.wait_ge(s_tanh, n + 1)
                link(dve.tensor_scalar(wa, th, 0.25, 0.25, ALU.mult, ALU.add), n, 12)
                link(dve.tensor_scalar(wb, th, -0.25, 0.25, ALU.mult, ALU.add), n, 13)
                link(dve.tensor_tensor(s1, s1, spread_e(wa), ALU.mult), n, 14)
                link(dve.tensor_tensor(s2, s2, spread_e(wb), ALU.mult), n, 15)
                link(dve.tensor_tensor(wsum, s1, s2, ALU.add), n, 16)
                link(dve.tensor_copy(w16[:, :, 0:E].bitcast(F32R), wsum), n, 17)
                dve.tensor_tensor(w16[:, :, E:2 * E], wsum, w16[:, :, 0:E], ALU.subtract).then_inc(s_w16, 1)

            def weights_copy(n, par):
                dve.wait_ge(s_wt, n + 1)
                dve.tensor_copy(wT[0:2 * E, bass.ds(par, 1), :], ps_r[0:2 * E, :]).then_inc(s_wT, 1)

            def scale_h(e, g, warm):
                dve.wait_ge(s_gelu, g + 1)
                dve.wait_ge(s_bc, g + 1)
                if warm:
                    dve.wait_ge(s_lo, g - HB + 1)
                w = ps_w.unsqueeze(1).broadcast_to([P, FH, BLK])
                dve.tensor_tensor(scaled_h[:, e % HB, :, :], gelu_h[:, e % 2, :, :], w, ALU.mult).then_inc(s_scaled, 1)

            def residual(b, n):
                dve.wait_ge(s_yt, n + 1)
                dve.tensor_tensor(xblk(b), ps_t[:], xblk(b), ALU.add).then_inc(s_xnew, 1)

            def xtile(b):
                return lambda j: x_res[:, bass.ds(b * TPB + j, 1), :].rearrange("p a d -> p (a d)")

            def ffn_block(layer, b, first, last):
                n = layer * NB + b
                cold = first and layer == 0
                for e in range(E):
                    g = n * E + e
                    if e == 7 and not last:
                        weights_copy(n + 1, (b + 1) % 2)
                    scale_h(e, g, not (cold and e < HB))
                    if not last:
                        if e == 0:
                            norm_stats(nf, 0, xtile(b + 1), n + 1)
                        if e == 1:
                            norm_apply(nf, 0, xtile(b + 1), xn_ffn, n + 1)
                        if e == 2:
                            norm_split(nf, b + 1, n + 1)
                        if e == 5:
                            top2(n + 1)
                        if e == 6:
                            expert_weights(n + 1)
                    if not first:
                        if e == 4:
                            residual(b - 1, n - 1)
                        if layer == 0:
                            if e == 4:
                                dve.wait_ge(s_xnew, n)
                                dve.memset(wait_pad[:], 0.0)
                                norm_stats(nm, 1, xtile(b - 1), b - 1)
                            if e == 6:
                                norm_apply(nm, 1, xtile(b - 1), xn_mix, b - 1)
                            if e == 7:
                                norm_split(nm, b - 1, b - 1)

            def ffn_layer(layer):
                ffn_block(layer, 0, True, False)
                with dve.Fori(1, NB - 1) as b:
                    ffn_block(layer, b, False, False)
                ffn_block(layer, NB - 1, False, True)
                n = layer * NB + NB - 1
                residual(NB - 1, n)
                if layer == 0:
                    dve.wait_ge(s_xnew, NB)
                    norm_stats(nm, 1, xtile(NB - 1), NB - 1)
                    norm_apply(nm, 1, xtile(NB - 1), xn_mix, NB - 1)
                    norm_split(nm, NB - 1, NB - 1)

            MIX_LINKS = 2 * NDU - 1

            def mix_gates(i, first):
                v = v_pad[:, bass.ds(i % 2, 1), :].rearrange("p a c -> p (a c)")
                k = 0
                dve.wait_ge(s_v, i + 1)
                for m, u in enumerate(DVE_UNITS):
                    if m == 0 and not first:
                        dve.wait_ge(s_mixed, i)
                    if m > 1:
                        dve.wait_ge(s_dl, i * (NDU - 1) + m - 1)
                    dve.wait_ge(s_gate, i * NS + u)
                    g = scaled_h[:, (u - 1) % HB, :, :].rearrange("p k c -> p (k c)")
                    vs = v[:, HALO + SHIFTS[u - 1]:HALO + SHIFTS[u - 1] + SEQ]
                    dve.tensor_tensor(acc_d if m == 0 else prod_d, g, vs, ALU.mult).then_inc(s_dg, 1)
                    if m > 0:
                        dve.wait_ge(s_dg, i * NDU + m + 1)
                        dve.tensor_tensor(acc_d, acc_d, prod_d, ALU.add).then_inc(s_dl, 1)
                    if m == 1 and not first:
                        mix_stats(i - 1)
                    if m == 2 and not first:
                        mix_bias(i - 1)
                    if m == 4 and not first:
                        mix_residual(i - 1)
                dve.wait_ge(s_dl, (i + 1) * (NDU - 1))
                dve.wait_ge(s_psum_p, i + 1)
                if not first:
                    dve.wait_ge(s_ot, i)
                dve.tensor_tensor(mixed[:], acc_d, acc_p, ALU.add).then_inc(s_mixed, 1)

            def mix_stats(i):
                dve.wait_ge(s_ot, i + 1)
                for j in range(TPS):
                    t = dve.bn_stats(stats_o[:, j, :], ps_out[:, j // TPB, (j % TPB) * P:(j % TPB + 1) * P])
                t.then_inc(s_ol, 1)
                dve.wait_ge(s_ol, i + 1)
                if not zero(i):
                    dve.wait_ge(s_z, i)
                dve.memset(wait_pad[:], 0.0)
                for j in range(TPS):
                    t = dve.bn_aggr(mv_o[:, j, :], stats_o[:, j, :])
                t.then_inc(s_ostat, 1)

            def mix_bias(i):
                dve.wait_ge(s_orstd, i + 1)
                dve.scalar_tensor_tensor(nbias_o[:], mv_o[:, :, 0], -1.0, rstd_o[:], ALU.mult, ALU.mult).then_inc(s_nb, 1)

            def mix_residual(i):
                dve.wait_ge(s_zg, i + 1)
                dve.wait_ge(s_xb, i + 1)
                xs = x_res[:, bass.ds(i * TPS, TPS), :]
                dve.tensor_tensor(xs, xs, z_mix[:], ALU.add).then_inc(s_xmix, 1)

            def mix_seq(i, first):
                mix_gates(i, first)

            for e in range(E):
                t = dve.memset(rank[:, :, e:e + 1], float(E - e))
            t.then_inc(s_rank, 1)
            dve.memset(lgT[:], 0.0).then_inc(s_pad, 1)
            dve.memset(wT[:].bitcast(F32), 0.0).then_inc(s_pad, 1)
            dve.wait_ge(s_x0, 16)
            norm_stats(nf, 0, lambda j: x_res[:, j, :], 0)
            dve.wait_ge(s_rtT, 1)
            dve.tensor_copy(rt_hi[:], ps_t[:, 0, 0:E]).then_inc(s_rts, 1)
            dve.wait_ge(s_rts, 1)
            dve.tensor_tensor(rt_lo[:], ps_t[:, 0, 0:E], rt_hi[:].bitcast(F32), ALU.subtract).then_inc(s_rts, 1)
            norm_apply(nf, 0, lambda j: x_res[:, j, :], xn_ffn, 0)
            norm_split(nf, 0, 0)
            dve.wait_ge(s_const, 2)
            dve.tensor_copy(sel[:], sel_raw[:]).then_inc(s_sel, 1)
            dve.wait_ge(s_mixh, 1)
            mix_pairs = ps_out[:, :, :].rearrange("p a c -> p (a c)").rearrange("p (u c) -> p u c", c=P)
            dve.tensor_tensor(mix_lo[:, 0:8, :], mix_pairs, mix_hi[:, 0:8, :].bitcast(F32), ALU.subtract).then_inc(s_mixl, 1)
            dve.wait_ge(s_rank, 1)
            top2(0)
            dve.wait_ge(s_mixh, 2)
            dve.tensor_tensor(mix_lo[:, 8:U, :], mix_pairs[:, 0:U - 8, :], mix_hi[:, 8:U, :].bitcast(F32), ALU.subtract).then_inc(s_mixl, 1)
            expert_weights(0)
            weights_copy(0, 0)
            dve.wait_ge(s_w1l, 1)
            dve.wait_ge(s_w2l, 1)
            dve.wait_ge(s_w1h, 1)
            dve.wait_ge(s_w2h, 1)
            dve.wait_ge(s_x1, 16)
            ffn_layer(0)
            mix_seq(0, True)
            with dve.Fori(1, BATCH) as i:
                mix_gates(i, False)
            dve.wait_ge(s_xmix, 1)
            norm_stats(nf, 0, xtile(0), NB)
            norm_apply(nf, 0, xtile(0), xn_ffn, NB)
            mix_stats(BATCH - 1)
            norm_split(nf, 0, NB)
            mix_bias(BATCH - 1)
            top2(NB)
            expert_weights(NB)
            weights_copy(NB, 0)
            mix_residual(BATCH - 1)
            dve.wait_ge(s_xmix, BATCH)
            ffn_layer(1)

        @block.gpsimd
        def _(pool):
            def norm_rstd(s, w, n):
                pool.wait_ge(s.stat, n + 1)
                pool.tensor_tensor(veps[:, w, :], mv[:, w, :, 1], eps_c[:, 0:TPB], ALU.add).then_inc(s.veps, 1)
                pool.wait_ge(s.veps, n + 1)
                pool.tensor_tensor(rstd[:, w, :], veps[:, w, :], m_half[:, 0:TPB], ALU.pow).then_inc(s.rstd, 1)

            def h_rest(e, g, warm):
                pool.wait_ge(s_hi, g + 1)
                if warm:
                    pool.wait_ge(s_down, g - HB + 1)
                pool.tensor_tensor(h_lo[:, e % HB, :, :], scaled_h[:, e % HB, :, :], h_hi[:, e % HB, :, :].bitcast(F32),
                                   ALU.subtract).then_inc(s_lo, 1)

            def ffn_block(layer, b, first, last):
                n = layer * NB + b
                cold = first and layer == 0
                for e in range(E):
                    g = n * E + e
                    if e == 1 and not last:
                        norm_rstd(nf, 0, n + 1)
                    if e == 6 and layer == 0 and not first:
                        norm_rstd(nm, 1, b - 1)
                    h_rest(e, g, not (cold and e < HB))

            def ffn_layer(layer):
                ffn_block(layer, 0, True, False)
                with pool.Fori(1, NB - 1) as b:
                    ffn_block(layer, b, False, False)
                ffn_block(layer, NB - 1, False, True)

            def mix_gates(i, first):
                v = v_pad[:, bass.ds(i % 2, 1), :].rearrange("p a c -> p (a c)")
                pool.wait_ge(s_v, i + 1)
                for m, u in enumerate(POOL_UNITS):
                    pool.wait_ge(s_gate, i * NS + u)
                    if m == 0 and not first:
                        pool.wait_ge(s_mixed, i)
                    if m > 1:
                        pool.wait_ge(s_pl, i * (NPU - 2) + m - 1)
                    g = scaled_h[:, (u - 1) % HB, :, :].rearrange("p k c -> p (k c)")
                    vs = v[:, HALO + SHIFTS[u - 1]:HALO + SHIFTS[u - 1] + SEQ]
                    pool.tensor_tensor(acc_p if m == 0 else prod_p, g, vs, ALU.mult).then_inc(s_pg, 1)
                    if m > 0:
                        pool.wait_ge(s_pg, i * NPU + m + 1)
                        t = pool.tensor_tensor(acc_p, acc_p, prod_p, ALU.add)
                        t.then_inc(s_psum_p if m == NPU - 1 else s_pl, 1)
                    if m == 0 and not first:
                        add_beta(i - 1)
                        out_rstd(i - 1)
                    if m == 1 and not first:
                        times_gamma(i - 1)

            def add_beta(i):
                xs = x_res[:, bass.ds(i * TPS, TPS), :]
                pool.tensor_tensor(xs, xs, beta_b[:].unsqueeze(1).broadcast_to([P, TPS, D]), ALU.add).then_inc(s_xb, 1)

            def out_rstd(i):
                pool.wait_ge(s_ostat, i + 1)
                pool.tensor_tensor(veps_o[:], mv_o[:, :, 1], eps_c[:], ALU.add).then_inc(s_oveps, 1)
                pool.wait_ge(s_oveps, i + 1)
                pool.tensor_tensor(rstd_o[:], veps_o[:], m_half[:], ALU.pow).then_inc(s_orstd, 1)

            def times_gamma(i):
                pool.wait_ge(s_z, i + 1)
                pool.tensor_tensor(z_mix[:], z_mix[:], gamma_b[:].unsqueeze(1).broadcast_to([P, TPS, D]), ALU.mult).then_inc(s_zg, 1)

            pool.memset(ident[:], 0.0)
            pool.memset(sel_raw[:], 0.0)
            pool.memset(eps_c[:], LN_EPS)
            pool.memset(m_half[:], -0.5).then_inc(s_zero, 1)
            pool.wait_ge(s_zero, 1)
            pool.affine_select(out=ident[:], in_=ident[:], compare_op=ALU.not_equal, fill=1.0,
                               base=0, pattern=[[-1, P]], channel_multiplier=1).then_inc(s_const, 1)
            norm_rstd(nf, 0, 0)
            for k in range(2):
                if k:
                    pool.wait_ge(s_zero, 2)
                t = pool.affine_select(out=sel_raw[:], in_=sel_raw[:], compare_op=ALU.not_equal, fill=1.0,
                                       base=-k * E, pattern=[[-1, E], [0, P]], channel_multiplier=1)
                t.then_inc(s_const if k else s_zero, 1)
            pool.wait_ge(s_w1h, 1)
            pool.tensor_tensor(w1_lo[:], w1_raw, w1_hi[:].bitcast(F32), ALU.subtract).then_inc(s_w1l, 1)
            pool.wait_ge(s_w2h, 1)
            pool.tensor_tensor(w2_lo[:], w2_raw, w2_hi[:].bitcast(F32), ALU.subtract).then_inc(s_w2l, 1)
            ffn_layer(0)
            norm_rstd(nm, 1, NB - 1)
            pool.wait_ge(s_gb, 32)
            pool.wait_ge(s_xnew, NB)
            mix_gates(0, True)
            with pool.Fori(1, BATCH) as i:
                mix_gates(i, False)
            add_beta(BATCH - 1)
            norm_rstd(nf, 0, NB)
            out_rstd(BATCH - 1)
            times_gamma(BATCH - 1)
            ffn_layer(1)


_INS = ['L0_attn_x', 'L0_attn_gate_W', 'L0_attn_value_W', 'L0_attn_gamma', 'L0_attn_beta', 'L0_ffn_router_w', 'L0_ffn_w1', 'L0_ffn_w2']


def kernel(**inputs):
    import numpy as _np
    import concourse.bacc as _bacc
    from concourse import mybir as _mybir
    from concourse.bass_utils import run_bass_kernel_spmd as _run

    nc = _bacc.Bacc("TRN2", target_bir_lowering=False, num_devices=1)
    arrays, args = {}, []
    for name in _INS:
        a = _np.ascontiguousarray(inputs[name])
        arrays[f"in_{name}_dram"] = a
        args.append(nc.dram_tensor(f"in_{name}_dram", a.shape, _mybir.dt.from_np(a.dtype), kind="ExternalInput").ap())
    shape = arrays["in_L0_attn_x_dram"].shape
    args.append(nc.dram_tensor("out_0_dram", shape, _mybir.dt.float32, kind="ExternalOutput").ap())
    macaron_program(nc, *args)
    r = _run(nc, [arrays], core_ids=[0])
    return r.results[0]["out_0_dram"]
```

```python
from contextlib import ExitStack

import concourse.bass as bass
from concourse import mybir

F32 = mybir.dt.float32
F32R = mybir.dt.float32r
ALU = mybir.AluOpType
ACT = mybir.ActivationFunctionType
AX_X = mybir.AxisListType.X

P = 128
SHIFTS = (0, -32, -16, -4, -1, 1, 4, 16, 32)
LN_EPS = 1e-05
BELOW_ALL = -3.0e38


def macaron_program(nc, x_in, gate_W, value_W, gamma, beta, router_w, w1, w2, out):
    BATCH, SEQ, D = x_in.shape
    E, _, FF = w1.shape
    T = BATCH * SEQ
    BLK = 512
    TPB = BLK // P
    NB = T // BLK
    BPS = SEQ // BLK
    FH = FF // P
    NS = len(SHIFTS)
    U = NS + 1
    HALO = max(SHIFTS)
    LAG = 3
    HB = 4
    TPS = SEQ // P
    assert D == P and FH == 2 and BPS == 2 and E % HB == 0 and LAG < HB and E == 8
    MIXW_ROUNDS = (range(0, 4), range(4, 8), range(8, U))
    MIXW_STEPS = (0, 1, 4)
    POOL_UNITS = (2, 5, 8)
    DVE_UNITS = tuple(u for u in range(1, U) if u not in POOL_UNITS)
    NPU, NDU = len(POOL_UNITS), len(DVE_UNITS)

    x_tiles = x_in.rearrange("b s d -> (b s) d").rearrange("(n p) d -> p n d", p=P)
    out_tiles = out.rearrange("b s d -> (b s) d").rearrange("(n p) d -> p n d", p=P)

    def zero(n):
        return isinstance(n, int) and n == 0

    with ExitStack() as ctx:
        def sb(name, shape, dt=F32):
            return ctx.enter_context(nc.sbuf_tensor(name, shape, dt))

        def psum(name, shape):
            return ctx.enter_context(nc.psum_tensor(name, shape, F32))

        def sem(name):
            return ctx.enter_context(nc.semaphore(name))

        x_res = sb("x_res", [P, NB * TPB, D])
        xT_hi = sb("xT_hi", [P, NB, BLK], F32R)
        xT_lo = sb("xT_lo", [P, NB, BLK], F32R)
        w1_hi = sb("w1_hi", [P, E, FF], F32R)
        w1_lo = sb("w1_lo", [P, E, FF], F32R)
        w2_hi = sb("w2_hi", [P, E, FH, D], F32R)
        w2_lo = sb("w2_lo", [P, E, FH, D], F32R)
        mix_hi = sb("mix_hi", [P, U, P], F32R)
        mix_lo = sb("mix_lo", [P, U, P], F32R)
        rt_hi = sb("rt_hi", [P, E], F32R)
        rt_lo = sb("rt_lo", [P, E], F32R)
        gelu_h = sb("gelu_h", [P, 2, FH, BLK])
        scaled_h = sb("scaled_h", [P, HB, FH, BLK])
        h_hi = sb("h_hi", [P, HB, FH, BLK], F32R)
        h_lo = sb("h_lo", [P, HB, FH, BLK], F32R)
        pool_mix = sb("pool_mix", [P, 2, SEQ])
        v_pad = sb("v_pad", [P, 2, SEQ + 2 * HALO])
        mixed = sb("mixed", [P, SEQ])
        z_mix = sb("z_mix", [P, TPS, D])
        xn_ffn = sb("xn_ffn", [P, TPB, D])
        xn_mix = sb("xn_mix", [P, TPB, D])
        yT = sb("yT", [P, BLK])
        lgT = sb("lgT", [P, BLK])
        wT = sb("wT", [P, 2, BLK], F32R)
        sel = sb("sel", [P, E, P], F32R)
        sel_raw = sb("sel_raw", [P, E, P])
        rt_raw = sb("rt_raw", [E, D])
        ident = sb("ident", [P, P])
        gamma_b = sb("gamma_b", [P, D])
        beta_b = sb("beta_b", [P, D])
        stats = sb("stats", [P, 2, TPB, 6])
        mv = sb("mv", [P, 2, TPB, 2])
        veps = sb("veps", [P, 2, TPB])
        rstd = sb("rstd", [P, 2, TPB])
        stats_o = sb("stats_o", [P, TPS, 6])
        mv_o = sb("mv_o", [P, TPS, 2])
        veps_o = sb("veps_o", [P, TPS])
        rstd_o = sb("rstd_o", [P, TPS])
        nbias_o = sb("nbias_o", [P, TPS])
        m_half = sb("m_half", [P, TPS])
        eps_c = sb("eps_c", [P, TPS])
        wait_pad = sb("wait_pad", [P, 1])
        rank = sb("rank", [P, TPB, E])
        top = sb("top", [P, 8, TPB])
        pick = sb("pick", [P, 6, TPB, E])
        w16 = sb("w16", [P, TPB, 2 * E])

        ps_up = psum("ps_up", [P, 2, FH, BLK])
        ps_out = psum("ps_out", [P, 2, BLK])
        ps_t = psum("ps_t", [P, TPB, P])
        ps_r = psum("ps_r", [P, BLK])
        ps_y, ps_w = ps_out[:, 0, :], ps_out[:, 1, :]
        logits = ps_r[:, :].rearrange("p (t c) -> p t c", c=P)[:, :, 0:E]

        w1_raw = scaled_h[:, 0:2, :, :].rearrange("p a k c -> p (a k c)").rearrange("p (e f) -> p e f", e=E)
        w2_raw = scaled_h[:, 2:4, :, :].rearrange("p a k c -> p (a k c)").rearrange("p (e k d) -> p e k d", e=E, k=FH)
        mix_raw = pool_mix[:, :, :].rearrange("p a c -> p (a c)")[:, 0:U * D].rearrange("p (u d) -> p u d", u=U)
        acc_d, prod_d = gelu_h[:, 0, :, :].rearrange("p k c -> p (k c)"), gelu_h[:, 1, :, :].rearrange("p k c -> p (k c)")
        acc_p, prod_p = pool_mix[:, 0, :], pool_mix[:, 1, :]

        s_x0, s_x1, s_w1, s_w2, s_rt, s_mixw, s_gb = (sem(n) for n in ("x0_in", "x1_in", "w1_in", "w2_in", "rt_in", "mixw_in", "gb_in"))
        s_zero, s_const = sem("consts_cleared"), sem("consts_ready")
        s_sel, s_rank, s_pad = sem("sel_ready"), sem("rank_ready"), sem("rows_cleared")
        s_rtT, s_rts = sem("router_turned"), sem("router_split")
        s_w1h, s_w1l, s_w2h, s_w2l = (sem(n) for n in ("w1_hi_ready", "w1_lo_ready", "w2_hi_ready", "w2_lo_ready"))
        s_mixT, s_mixh, s_mixl = sem("mixw_turned"), sem("mixw_hi_ready"), sem("mixw_lo_ready")

        class Norm:
            def __init__(self, n):
                self.link, self.stat, self.veps, self.rstd, self.xn, self.turned, self.split = (
                    sem(f"{n}_{k}") for k in ("link", "stats_ready", "veps_ready", "rstd_ready", "xn_ready", "turned", "split"))
        nf, nm = Norm("ffn"), Norm("mix")
        s_lg, s_lgT, s_lgt = sem("logitsT_ready"), sem("logitsT_copied"), sem("logits_ready")
        s_tl, s_gap, s_tanh, s_w16, s_wt, s_wT = (sem(n) for n in ("top_link", "gap_ready", "tanh_ready", "w16_ready", "wT_turned", "wT_ready"))
        s_up, s_bc, s_gelu, s_scaled, s_hi, s_lo, s_down = (
            sem(n) for n in ("up_done", "weights_spread", "gelu_done", "scaled_done", "h_hi_done", "h_lo_done", "down_done"))
        s_yT, s_yt, s_xnew = sem("yT_copied"), sem("y_turned"), sem("x_updated")
        s_mm, s_v, s_gate, s_dg, s_pg, s_dl, s_pl = (
            sem(n) for n in ("mix_product_done", "value_copied", "gate_ready", "dve_gate_used", "pool_gate_used", "dve_mix_link", "pool_mix_link"))
        s_psum_p, s_mixed, s_ot, s_ol, s_ostat, s_oveps, s_orstd, s_nb, s_z, s_zg, s_xb, s_xmix = (
            sem(n) for n in ("pool_sum_ready", "mixed_ready", "mixed_turned", "out_link", "out_stats_ready", "out_veps_ready",
                             "out_rstd_ready", "out_bias_ready", "z_ready", "z_gamma_ready", "x_beta_ready", "x_mixed"))
        s_out = sem("out_stored")

        def xblk(b):
            return x_res[:, bass.ds(b * TPB, TPB), :]

        block = ctx.enter_context(nc.Block())

        @block.sync
        def _(sp):
            sp.dma_start(x_res[:, 0:TPB, :], x_tiles[:, 0:TPB, :]).then_inc(s_x0, 16)
            sp.dma_start(w1_raw, w1.rearrange("e d f -> d e f")).then_inc(s_w1, 16)
            sp.dma_start(rt_raw[:], router_w).then_inc(s_rt, 16)
            sp.dma_start(w2_raw, w2.rearrange("e (k p) d -> p e k d", p=P)).then_inc(s_w2, 16)
            sp.dma_start(mix_raw[:, 0:1, :], value_W.rearrange("(u e) d -> e u d", e=P)).then_inc(s_mixw, 16)
            sp.dma_start(mix_raw[:, 1:U, :], gate_W.rearrange("(u e) d -> e u d", e=P)).then_inc(s_mixw, 16)
            sp.dma_start(x_res[:, TPB:, :], x_tiles[:, TPB:, :]).then_inc(s_x1, 16)
            sp.dma_start(gamma_b[:], gamma.rearrange("(a d) -> a d", a=1).partition_broadcast(P)).then_inc(s_gb, 16)
            sp.dma_start(beta_b[:], beta.rearrange("(a d) -> a d", a=1).partition_broadcast(P)).then_inc(s_gb, 16)
            with sp.Fori(0, NB) as b:
                sp.wait_ge(s_xnew, b + NB + 1)
                sp.dma_start(out_tiles[:, bass.ds(b * TPB, TPB), :], xblk(b)).then_inc(s_out, 16)
            sp.wait_ge(s_out, 16 * NB)

        @block.tensor
        def _(pe):
            def turn_x(s, xn, n, free):
                pe.wait_ge(s.xn, n + 1)
                for sm, v in free:
                    pe.wait_ge(sm, v)
                for j in range(TPB):
                    t = pe.transpose(ps_t[:, j, :], xn[:, j, :], ident[:])
                t.then_inc(s.turned, 1)

            def router(b, n):
                pe.wait_ge(nf.split, 2 * n + 2)
                if not zero(n):
                    pe.wait_ge(s_wT, n)
                pe.matmul(ps_r[0:E, :], rt_hi[:], xT_hi[:, bass.ds(b, 1), :], start=True, stop=False)
                pe.matmul(ps_r[0:E, :], rt_hi[:], xT_lo[:, bass.ds(b, 1), :], start=False, stop=False)
                pe.matmul(ps_r[0:E, :], rt_lo[:], xT_hi[:, bass.ds(b, 1), :], start=False, stop=True).then_inc(s_lg, 1)

            def turn_logits(n):
                pe.wait_ge(s_lgT, n + 1)
                for j in range(TPB):
                    t = pe.transpose(ps_r[:, j * P:(j + 1) * P], lgT[:, j * P:(j + 1) * P], ident[:])
                t.then_inc(s_lgt, 1)

            def turn_weights(n):
                pe.wait_ge(s_w16, n + 1)
                for j in range(TPB):
                    t = pe.transpose(ps_r[0:2 * E, j * P:(j + 1) * P], w16[:, j, :], ident[:])
                t.then_inc(s_wt, 1)

            def up(b, e, g, warm):
                if warm:
                    pe.wait_ge(s_gelu, g - 1)
                for k in range(FH):
                    w = slice(k * P, (k + 1) * P)
                    pe.matmul(ps_up[:, e % 2, k, :], w1_hi[:, e, w], xT_hi[:, bass.ds(b, 1), :], start=True, stop=False)
                    pe.matmul(ps_up[:, e % 2, k, :], w1_hi[:, e, w], xT_lo[:, bass.ds(b, 1), :], start=False, stop=False)
                    t = pe.matmul(ps_up[:, e % 2, k, :], w1_lo[:, e, w], xT_hi[:, bass.ds(b, 1), :], start=False, stop=True)
                t.then_inc(s_up, 1)

            def spread(e, g, n, par):
                if e == 0:
                    pe.wait_ge(s_wT, n + 1)
                if not zero(g):
                    pe.wait_ge(s_scaled, g)
                pe.matmul(ps_w, sel[:, e, :], wT[:, bass.ds(par, 1), :], start=True, stop=True).then_inc(s_bc, 1)

            def down(e, g, n):
                pe.wait_ge(s_hi, g + 1)
                pe.wait_ge(s_lo, g + 1)
                if e == 0 and not zero(n):
                    pe.wait_ge(s_yT, n)
                for k in range(FH):
                    pe.matmul(ps_y, w2_hi[:, e, k, :], h_hi[:, e % HB, k, :], start=(e == 0 and k == 0), stop=False)
                    pe.matmul(ps_y, w2_lo[:, e, k, :], h_hi[:, e % HB, k, :], start=False, stop=False)
                    t = pe.matmul(ps_y, w2_hi[:, e, k, :], h_lo[:, e % HB, k, :], start=False, stop=(e == E - 1 and k == FH - 1))
                t.then_inc(s_down, 1)

            def turn_y(n, free):
                pe.wait_ge(s_yT, n + 1)
                for sm, v in free:
                    pe.wait_ge(sm, v)
                for j in range(TPB):
                    t = pe.transpose(ps_t[:, j, :], yT[:, j * P:(j + 1) * P], ident[:])
                t.then_inc(s_yt, 1)

            def ffn_block(layer, b, first, last, second=False):
                n = layer * NB + b
                cold = first and layer == 0
                for e in range(E):
                    g = n * E + e
                    if first and e == 0:
                        pe.wait_ge(nf.split, 2 * n + 2)
                    if cold and e % 2 == 0:
                        pe.wait_ge(s_w1l, e // 2 + 1)
                    up(b, e, g, not (cold and e < 2))
                    if cold and e == 0:
                        turn_weights(0)
                    if cold and e in MIXW_STEPS:
                        turn_mix_weights(MIXW_STEPS.index(e))
                    if e == 4 and not last:
                        turn_logits(n + 1)
                    if e >= LAG:
                        if cold and (e - LAG) % 2 == 0:
                            pe.wait_ge(s_w2l, (e - LAG) // 2 + 1)
                        down(e - LAG, g - LAG, n)
                    elif not first:
                        down(e - LAG + E, g - LAG, n - 1)
                    if e == 2 and not last:
                        if cold:
                            free = [(s_mixl, 2)]
                        elif second and layer == 0:
                            free = [(s_mixl, 3)]
                        elif first or second:
                            free = []
                        else:
                            free = [(nm.split, 2 * b - 2)] if layer == 0 else [(s_xnew, n - 1)]
                        turn_x(nf, xn_ffn, n + 1, free)
                    if e == 3 and not first:
                        if not last:
                            free = [(nf.split, 2 * n + 4)]
                        else:
                            free = [(nm.split, 2 * b - 2)] if layer == 0 else [(s_xnew, n - 1)]
                        turn_y(n - 1, free)
                    if e == 3 and not last:
                        router(b + 1, n + 1)
                    if e == 6 and layer == 0 and not first:
                        turn_x(nm, xn_mix, b - 1, [(s_xnew, b)])
                    if layer == 1 and first and e == 0:
                        pe.wait_ge(s_z, BATCH)
                    spread(e, g, n, b % 2)
                    if e == 7 and not last:
                        turn_weights(n + 1)

            def ffn_layer(layer):
                ffn_block(layer, 0, True, False)
                if layer == 0:
                    ffn_block(layer, 1, False, False, second=True)
                with pe.Fori(2 - layer, NB - 1) as b:
                    ffn_block(layer, b, False, False)
                ffn_block(layer, NB - 1, False, True)
                n = layer * NB + NB - 1
                for e in range(E - LAG, E):
                    down(e, n * E + e, n)
                if layer == 1:
                    turn_y(n, [(s_xnew, n)])

            def turn_mix_weights(r):
                if r == 0:
                    pe.wait_ge(s_mixw, 32)
                elif r == 1:
                    pe.wait_ge(s_mixl, 1)
                else:
                    pe.wait_ge(nf.split, 4)
                for k, u in enumerate(MIXW_ROUNDS[r]):
                    t = pe.transpose(ps_t[:, k, :], mix_raw[:, u, :], ident[:])
                t.then_inc(s_mixT, 1)

            def turn_mixed(i):
                pe.wait_ge(s_mixed, i + 1)
                if not zero(i):
                    pe.wait_ge(s_z, i)
                for j in range(TPS):
                    t = pe.transpose(ps_out[:, j // TPB, (j % TPB) * P:(j % TPB + 1) * P], mixed[:, j * P:(j + 1) * P], ident[:])
                t.then_inc(s_ot, 1)

            def mix_seq(i, first, last=False):
                for u in range(U):
                    if first and u == 2:
                        turn_y(NB - 1, [(nm.split, 2 * NB - 2)])
                    if first and u == 7:
                        turn_x(nm, xn_mix, NB - 1, [(s_xnew, NB)])
                    if last and u == 7:
                        turn_x(nf, xn_ffn, NB, [])
                    if last and u == 9:
                        router(0, NB)
                    q = i * U + u
                    if not (first and u < 2):
                        if u == 0:
                            pe.wait_ge(s_gate, i * NS - 1)
                        elif u == 1:
                            pe.wait_ge(s_gate, i * NS)
                        elif u == 2:
                            pe.wait_ge(s_v, i + 1)
                        else:
                            pe.wait_ge(s_gate, i * NS + u - 2)
                    for k in range(BPS):
                        if u == 0:
                            pe.wait_ge(nm.split, 4 * i + 2 * k + 2)
                        xb = bass.ds(i * BPS + k, 1)
                        pe.matmul(ps_up[:, u % 2, k, :], mix_hi[:, u, :], xT_hi[:, xb, :], start=True, stop=False)
                        pe.matmul(ps_up[:, u % 2, k, :], mix_hi[:, u, :], xT_lo[:, xb, :], start=False, stop=False)
                        t = pe.matmul(ps_up[:, u % 2, k, :], mix_lo[:, u, :], xT_hi[:, xb, :], start=False, stop=True)
                    t.then_inc(s_mm, 1)
                    if u == 4 and not first:
                        turn_mixed(i - 1)

            pe.wait_ge(s_const, 1)
            pe.wait_ge(s_rt, 16)
            pe.transpose(ps_t[:, 0, 0:E], rt_raw[:], ident[0:E, 0:E]).then_inc(s_rtT, 1)
            turn_x(nf, xn_ffn, 0, [(s_rts, 2)])
            router(0, 0)
            turn_logits(0)
            pe.wait_ge(s_sel, 1)
            ffn_layer(0)
            mix_seq(0, True)
            with pe.Fori(1, BATCH - 1) as i:
                mix_seq(i, False)
            mix_seq(BATCH - 1, False, last=True)
            turn_logits(NB)
            turn_mixed(BATCH - 1)
            turn_weights(NB)
            ffn_layer(1)

        @block.scalar
        def _(act):
            def logits_copy(n):
                if zero(n):
                    act.wait_ge(s_pad, 2)
                act.wait_ge(s_lg, n + 1)
                act.activation(lgT[0:E, :], ps_r[0:E, :], ACT.Copy).then_inc(s_lgT, 1)

            def gap_tanh(n):
                act.wait_ge(s_gap, n + 1)
                act.activation(top[:, 5, :], top[:, 4, :], ACT.Tanh, scale=0.5).then_inc(s_tanh, 1)

            def norm_round(s, b, n):
                act.wait_ge(s.turned, n + 1)
                act.activation(xT_hi[:, bass.ds(b, 1), :], ps_t[:], ACT.Copy).then_inc(s.split, 1)

            def weights_copy(n, par):
                act.wait_ge(s_wt, n + 1)
                act.activation(wT[0:2 * E, bass.ds(par, 1), :], ps_r[0:2 * E, :], ACT.Copy).then_inc(s_wT, 1)

            def gelu(e, g, warm):
                act.wait_ge(s_up, g + 1)
                if warm:
                    act.wait_ge(s_scaled, g - 1)
                act.activation(gelu_h[:, e % 2, :, :], ps_up[:, e % 2, :, :], ACT.Gelu).then_inc(s_gelu, 1)

            def h_round(e, g, warm):
                act.wait_ge(s_scaled, g + 1)
                if warm:
                    act.wait_ge(s_down, g - HB + 1)
                act.activation(h_hi[:, e % HB, :, :], scaled_h[:, e % HB, :, :], ACT.Copy).then_inc(s_hi, 1)

            def y_copy(n):
                act.wait_ge(s_down, (n + 1) * E)
                if not zero(n):
                    act.wait_ge(s_yt, n)
                act.activation(yT[:], ps_y, ACT.Copy).then_inc(s_yT, 1)

            def ffn_block(layer, b, first, last):
                n = layer * NB + b
                cold = first and layer == 0
                for e in range(E):
                    g = n * E + e
                    if e == 0 and not first:
                        weights_copy(n, b % 2)
                    if e == 3 and not last:
                        norm_round(nf, b + 1, n + 1)
                    if e == LAG and not first:
                        y_copy(n - 1)
                    if e == 4 and not last:
                        logits_copy(n + 1)
                    if e == 7 and layer == 0 and not first:
                        norm_round(nm, b - 1, b - 1)
                    if cold and e - 1 in MIXW_STEPS:
                        mix_weights_round(MIXW_STEPS.index(e - 1))
                    gelu(e, g, not (cold and e < 2))
                    if layer == 1 and first and e == 0:
                        normalise_out(BATCH - 1)
                    if cold and e == 0:
                        weights_copy(0, 0)
                    if e == 6 and not last:
                        gap_tanh(n + 1)
                    if e >= 1:
                        h_round(e - 1, g - 1, not (cold and e - 1 < HB))
                    elif not first:
                        h_round(E - 1, g - 1, True)

            def ffn_layer(layer):
                ffn_block(layer, 0, True, False)
                with act.Fori(1, NB - 1) as b:
                    ffn_block(layer, b, False, False)
                ffn_block(layer, NB - 1, False, True)
                n = layer * NB + NB - 1
                h_round(E - 1, n * E + E - 1, True)
                y_copy(n)

            def mix_weights_round(r):
                us = MIXW_ROUNDS[r]
                act.wait_ge(s_mixT, r + 1)
                act.activation(mix_hi[:, us[0]:us[-1] + 1, :], ps_t[:, 0:len(us), :], ACT.Copy).then_inc(s_mixh, 1)

            def normalise_out(i):
                act.wait_ge(s_nb, i + 1)
                act.wait_ge(s_ot, i + 1)
                if not zero(i):
                    act.wait_ge(s_xmix, i)
                for j in range(TPS):
                    t = act.activation(z_mix[:, j, :], ps_out[:, j // TPB, (j % TPB) * P:(j % TPB + 1) * P], ACT.Identity,
                                       bias=nbias_o[:, j:j + 1], scale=rstd_o[:, j:j + 1])
                t.then_inc(s_z, 1)

            def gate(i, u, first):
                act.wait_ge(s_mm, i * U + u + 1)
                prev, turn = (u - HB, 0) if u > HB else ({1: 9, 2: 6, 3: 7, 4: 8}[u], 1)
                if not (first and turn):
                    if prev in POOL_UNITS:
                        act.wait_ge(s_pg, (i - turn) * NPU + POOL_UNITS.index(prev) + 1)
                    else:
                        act.wait_ge(s_dg, (i - turn) * NDU + DVE_UNITS.index(prev) + 1)
                act.activation(scaled_h[:, (u - 1) % HB, :, :], ps_up[:, u % 2, :, :], ACT.Sigmoid).then_inc(s_gate, 1)

            def value_copy(i, first):
                act.wait_ge(s_mm, i * U + 1)
                v = v_pad[:, bass.ds(i % 2, 1), :].rearrange("p a c -> p (a c)")
                pv = ps_up[:, 0, :, :].rearrange("p k c -> p (k c)")
                act.activation(v[:, HALO:HALO + SEQ], pv, ACT.Copy)
                act.activation(v[:, 0:HALO], pv[:, SEQ - HALO:SEQ], ACT.Copy)
                act.activation(v[:, HALO + SEQ:], pv[:, 0:HALO], ACT.Copy).then_inc(s_v, 1)

            def mix_seq(i, first, last=False):
                value_copy(i, first)
                for u in range(1, U):
                    gate(i, u, first)
                    if first and u == 7:
                        norm_round(nm, NB - 1, NB - 1)
                    if last and u == 7:
                        norm_round(nf, 0, NB)
                if last:
                    logits_copy(NB)
                if not first:
                    normalise_out(i - 1)
                if last:
                    gap_tanh(NB)
                    weights_copy(NB, 0)

            act.wait_ge(s_w1, 16)
            act.activation(w1_hi[:, 0:2, :], w1_raw[:, 0:2, :], ACT.Copy).then_inc(s_w1h, 1)
            act.activation(w1_hi[:, 2:E, :], w1_raw[:, 2:E, :], ACT.Copy).then_inc(s_w1h, 1)
            norm_round(nf, 0, 0)
            logits_copy(0)
            gap_tanh(0)
            ffn_layer(0)
            act.wait_ge(s_lo, NB * E)
            mix_seq(0, True)
            with act.Fori(1, BATCH - 1) as i:
                mix_seq(i, False)
            mix_seq(BATCH - 1, False, last=True)
            ffn_layer(1)

        @block.vector
        def _(dve):
            def norm_stats(s, w, xb, n):
                for j in range(TPB):
                    t = dve.bn_stats(stats[:, w, j, :], xb(j))
                t.then_inc(s.link, 1)
                dve.wait_ge(s.link, n + 1)
                dve.memset(wait_pad[:], 0.0)
                for j in range(TPB):
                    t = dve.bn_aggr(mv[:, w, j, :], stats[:, w, j, :])
                t.then_inc(s.stat, 1)

            def norm_apply(s, w, xb, xn, n):
                dve.wait_ge(s.rstd, n + 1)
                for j in range(TPB):
                    t = dve.tensor_scalar(xn[:, j, :], xb(j), mv[:, w, j, 0:1], rstd[:, w, j:j + 1], ALU.subtract, ALU.mult)
                t.then_inc(s.xn, 1)

            def norm_split(s, b, n):
                dve.wait_ge(s.split, 2 * n + 1)
                src = ps_t[:, :, :].rearrange("p j c -> p (j c)")
                hi = xT_hi[:, bass.ds(b, 1), :].rearrange("p a c -> p (a c)")
                lo = xT_lo[:, bass.ds(b, 1), :].rearrange("p a c -> p (a c)")
                dve.tensor_tensor(lo, src, hi.bitcast(F32), ALU.subtract).then_inc(s.split, 1)

            TOP_LINKS = 17

            def link(t, n, k):
                t.then_inc(s_tl, 1)
                dve.wait_ge(s_tl, TOP_LINKS * n + k)

            def spread_e(ap):
                return ap.unsqueeze(2).broadcast_to([P, TPB, E])

            def best(n):
                v1, r1, v2, r2, gap = (top[:, k, :] for k in range(5))
                k1, s1, lg2, k2, s2 = (pick[:, k, :, :] for k in range(5))
                dve.wait_ge(s_lgt, n + 1)
                link(dve.tensor_reduce(v1, logits, AX_X, ALU.max), n, 1)
                link(dve.tensor_tensor(k1, logits, spread_e(v1), ALU.is_equal), n, 2)
                link(dve.tensor_tensor(k1, k1, rank[:], ALU.mult), n, 3)
                link(dve.tensor_reduce(r1, k1, AX_X, ALU.max), n, 4)
                link(dve.tensor_tensor(s1, k1, spread_e(r1), ALU.is_equal), n, 5)
                link(dve.scalar_tensor_tensor(lg2, s1, BELOW_ALL, logits, ALU.mult, ALU.add), n, 6)

            def second_best(n):
                v1, r1, v2, r2, gap = (top[:, k, :] for k in range(5))
                k1, s1, lg2, k2, s2 = (pick[:, k, :, :] for k in range(5))
                link(dve.tensor_reduce(v2, lg2, AX_X, ALU.max), n, 7)
                dve.tensor_tensor(gap, v1, v2, ALU.subtract).then_inc(s_gap, 1)
                link(dve.tensor_tensor(k2, lg2, spread_e(v2), ALU.is_equal), n, 8)
                link(dve.tensor_tensor(k2, k2, rank[:], ALU.mult), n, 9)
                link(dve.tensor_reduce(r2, k2, AX_X, ALU.max), n, 10)
                link(dve.tensor_tensor(s2, k2, spread_e(r2), ALU.is_equal), n, 11)

            def expert_weights(n):
                th, wa, wb = (top[:, k, :] for k in (5, 6, 7))
                s1, s2, wsum = pick[:, 1, :, :], pick[:, 4, :, :], pick[:, 5, :, :]
                dve.wait_ge(s_tanh, n + 1)
                link(dve.tensor_scalar(wa, th, 0.25, 0.25, ALU.mult, ALU.add), n, 12)
                link(dve.tensor_scalar(wb, th, -0.25, 0.25, ALU.mult, ALU.add), n, 13)
                link(dve.tensor_tensor(s1, s1, spread_e(wa), ALU.mult), n, 14)
                link(dve.tensor_tensor(s2, s2, spread_e(wb), ALU.mult), n, 15)
                link(dve.tensor_tensor(wsum, s1, s2, ALU.add), n, 16)
                link(dve.tensor_copy(w16[:, :, 0:E].bitcast(F32R), wsum), n, 17)
                dve.tensor_tensor(w16[:, :, E:2 * E], wsum, w16[:, :, 0:E], ALU.subtract).then_inc(s_w16, 1)

            def mix_weights_rest(r):
                us = MIXW_ROUNDS[r]
                w = slice(us[0], us[-1] + 1)
                dve.wait_ge(s_mixh, r + 1)
                dve.tensor_tensor(mix_lo[:, w, :], ps_t[:, 0:len(us), :], mix_hi[:, w, :].bitcast(F32), ALU.subtract).then_inc(s_mixl, 1)

            def scale_h(e, g, warm):
                dve.wait_ge(s_gelu, g + 1)
                dve.wait_ge(s_bc, g + 1)
                if warm:
                    dve.wait_ge(s_lo, g - HB + 1)
                w = ps_w.unsqueeze(1).broadcast_to([P, FH, BLK])
                dve.tensor_tensor(scaled_h[:, e % HB, :, :], gelu_h[:, e % 2, :, :], w, ALU.mult).then_inc(s_scaled, 1)

            def residual(b, n):
                dve.wait_ge(s_yt, n + 1)
                dve.tensor_tensor(xblk(b), ps_t[:], xblk(b), ALU.add).then_inc(s_xnew, 1)

            def xtile(b):
                return lambda j: x_res[:, bass.ds(b * TPB + j, 1), :].rearrange("p a d -> p (a d)")

            def ffn_block(layer, b, first, last):
                n = layer * NB + b
                cold = first and layer == 0
                for e in range(E):
                    g = n * E + e
                    if cold and e == 0:
                        dve.wait_ge(s_w1l, E // 2)
                    if cold and e == 2:
                        dve.wait_ge(s_w2l, E // 2)
                    scale_h(e, g, not (cold and e < HB))
                    if not last:
                        if e == 0:
                            if cold:
                                dve.wait_ge(s_x1, 16)
                            norm_stats(nf, 0, xtile(b + 1), n + 1)
                        if e == 1:
                            norm_apply(nf, 0, xtile(b + 1), xn_ffn, n + 1)
                        if e == 2:
                            norm_split(nf, b + 1, n + 1)
                        if e == 4:
                            best(n + 1)
                    if e == 3 and not first:
                        residual(b - 1, n - 1)
                    if layer == 0 and not first:
                        if e == 3:
                            dve.wait_ge(s_xnew, n)
                            dve.memset(wait_pad[:], 0.0)
                            norm_stats(nm, 1, xtile(b - 1), b - 1)
                        if e == 5:
                            norm_apply(nm, 1, xtile(b - 1), xn_mix, b - 1)
                        if e == 7:
                            norm_split(nm, b - 1, b - 1)
                    if not last:
                        if e == 5:
                            second_best(n + 1)
                        if e == 6:
                            expert_weights(n + 1)
                    if cold and e in MIXW_STEPS:
                        mix_weights_rest(MIXW_STEPS.index(e))
                    if layer == 1 and first and e == 4:
                        mix_residual(BATCH - 1)

            def ffn_layer(layer):
                ffn_block(layer, 0, True, False)
                with dve.Fori(1, NB - 1) as b:
                    ffn_block(layer, b, False, False)
                ffn_block(layer, NB - 1, False, True)
                n = layer * NB + NB - 1
                if layer == 1:
                    residual(NB - 1, n)

            def mix_gates(i, first, last=False):
                v = v_pad[:, bass.ds(i % 2, 1), :].rearrange("p a c -> p (a c)")
                dve.wait_ge(s_v, i + 1)
                for m, u in enumerate(DVE_UNITS):
                    if m == 0 and not first:
                        dve.wait_ge(s_mixed, i)
                    if m > 1:
                        dve.wait_ge(s_dl, i * (NDU - 1) + m - 1)
                    dve.wait_ge(s_gate, i * NS + u)
                    g = scaled_h[:, (u - 1) % HB, :, :].rearrange("p k c -> p (k c)")
                    vs = v[:, HALO + SHIFTS[u - 1]:HALO + SHIFTS[u - 1] + SEQ]
                    dve.tensor_tensor(acc_d if m == 0 else prod_d, g, vs, ALU.mult).then_inc(s_dg, 1)
                    if m > 0:
                        dve.wait_ge(s_dg, i * NDU + m + 1)
                        dve.tensor_tensor(acc_d, acc_d, prod_d, ALU.add).then_inc(s_dl, 1)
                    if m == 1 and not first:
                        mix_stats(i - 1)
                    if m == 3 and not first:
                        mix_bias(i - 1)
                    if last:
                        if m == 0:
                            norm_stats(nf, 0, xtile(0), NB)
                        if m == 2:
                            norm_apply(nf, 0, xtile(0), xn_ffn, NB)
                        if m == 4:
                            norm_split(nf, 0, NB)
                    if first:
                        if m == 0:
                            residual(NB - 1, NB - 1)
                        if m == 1:
                            dve.wait_ge(s_xnew, NB)
                            norm_stats(nm, 1, xtile(NB - 1), NB - 1)
                        if m == 3:
                            norm_apply(nm, 1, xtile(NB - 1), xn_mix, NB - 1)
                        if m == 4:
                            norm_split(nm, NB - 1, NB - 1)
                dve.wait_ge(s_dl, (i + 1) * (NDU - 1))
                dve.wait_ge(s_psum_p, i + 1)
                if not first:
                    dve.wait_ge(s_ot, i)
                dve.tensor_tensor(mixed[:], acc_d, acc_p, ALU.add).then_inc(s_mixed, 1)
                if not first:
                    mix_residual(i - 1)

            def mix_stats(i):
                dve.wait_ge(s_ot, i + 1)
                for j in range(TPS):
                    t = dve.bn_stats(stats_o[:, j, :], ps_out[:, j // TPB, (j % TPB) * P:(j % TPB + 1) * P])
                t.then_inc(s_ol, 1)
                dve.wait_ge(s_ol, i + 1)
                if not zero(i):
                    dve.wait_ge(s_z, i)
                dve.memset(wait_pad[:], 0.0)
                for j in range(TPS):
                    t = dve.bn_aggr(mv_o[:, j, :], stats_o[:, j, :])
                t.then_inc(s_ostat, 1)

            def mix_bias(i):
                dve.wait_ge(s_orstd, i + 1)
                dve.scalar_tensor_tensor(nbias_o[:], mv_o[:, :, 0], -1.0, rstd_o[:], ALU.mult, ALU.mult).then_inc(s_nb, 1)

            def mix_residual(i):
                dve.wait_ge(s_zg, i + 1)
                dve.wait_ge(s_xb, i + 1)
                xs = x_res[:, bass.ds(i * TPS, TPS), :]
                dve.tensor_tensor(xs, xs, z_mix[:], ALU.add).then_inc(s_xmix, 1)

            for e in range(E):
                t = dve.memset(rank[:, :, e:e + 1], float(E - e))
            t.then_inc(s_rank, 1)
            dve.memset(lgT[:], 0.0).then_inc(s_pad, 1)
            dve.memset(wT[:].bitcast(F32), 0.0).then_inc(s_pad, 1)
            dve.wait_ge(s_x0, 16)
            norm_stats(nf, 0, lambda j: x_res[:, j, :], 0)
            dve.wait_ge(s_rtT, 1)
            dve.tensor_copy(rt_hi[:], ps_t[:, 0, 0:E]).then_inc(s_rts, 1)
            dve.wait_ge(s_rts, 1)
            dve.tensor_tensor(rt_lo[:], ps_t[:, 0, 0:E], rt_hi[:].bitcast(F32), ALU.subtract).then_inc(s_rts, 1)
            norm_apply(nf, 0, lambda j: x_res[:, j, :], xn_ffn, 0)
            dve.wait_ge(s_w2, 16)
            dve.tensor_copy(w2_hi[:], w2_raw).then_inc(s_w2h, 1)
            norm_split(nf, 0, 0)
            dve.wait_ge(s_const, 2)
            dve.tensor_copy(sel[:], sel_raw[:]).then_inc(s_sel, 1)
            dve.wait_ge(s_rank, 1)
            best(0)
            second_best(0)
            expert_weights(0)
            ffn_layer(0)
            mix_gates(0, True)
            with dve.Fori(1, BATCH - 1) as i:
                mix_gates(i, False)
            mix_gates(BATCH - 1, False, last=True)
            best(NB)
            second_best(NB)
            expert_weights(NB)
            mix_stats(BATCH - 1)
            mix_bias(BATCH - 1)
            ffn_layer(1)

        @block.gpsimd
        def _(pool):
            def norm_rstd(s, w, n):
                pool.wait_ge(s.stat, n + 1)
                pool.tensor_tensor(veps[:, w, :], mv[:, w, :, 1], eps_c[:, 0:TPB], ALU.add).then_inc(s.veps, 1)
                pool.wait_ge(s.veps, n + 1)
                pool.tensor_tensor(rstd[:, w, :], veps[:, w, :], m_half[:, 0:TPB], ALU.pow).then_inc(s.rstd, 1)

            def h_rest(e, g, warm):
                pool.wait_ge(s_hi, g + 1)
                if warm:
                    pool.wait_ge(s_down, g - HB + 1)
                pool.tensor_tensor(h_lo[:, e % HB, :, :], scaled_h[:, e % HB, :, :], h_hi[:, e % HB, :, :].bitcast(F32),
                                   ALU.subtract).then_inc(s_lo, 1)

            def ffn_block(layer, b, first, last):
                n = layer * NB + b
                cold = first and layer == 0
                for e in range(E):
                    g = n * E + e
                    if e == 0 and not last:
                        norm_rstd(nf, 0, n + 1)
                    if e == 4 and layer == 0 and not first:
                        norm_rstd(nm, 1, b - 1)
                    h_rest(e, g, not (cold and e < HB))

            def ffn_layer(layer):
                ffn_block(layer, 0, True, False)
                with pool.Fori(1, NB - 1) as b:
                    ffn_block(layer, b, False, False)
                ffn_block(layer, NB - 1, False, True)

            def mix_gates(i, first, last=False):
                v = v_pad[:, bass.ds(i % 2, 1), :].rearrange("p a c -> p (a c)")
                pool.wait_ge(s_v, i + 1)
                for m, u in enumerate(POOL_UNITS):
                    pool.wait_ge(s_gate, i * NS + u)
                    if m == 0 and not first:
                        pool.wait_ge(s_mixed, i)
                    if m > 1:
                        pool.wait_ge(s_pl, i * (NPU - 2) + m - 1)
                    g = scaled_h[:, (u - 1) % HB, :, :].rearrange("p k c -> p (k c)")
                    vs = v[:, HALO + SHIFTS[u - 1]:HALO + SHIFTS[u - 1] + SEQ]
                    pool.tensor_tensor(acc_p if m == 0 else prod_p, g, vs, ALU.mult).then_inc(s_pg, 1)
                    if m > 0:
                        pool.wait_ge(s_pg, i * NPU + m + 1)
                        t = pool.tensor_tensor(acc_p, acc_p, prod_p, ALU.add)
                        t.then_inc(s_psum_p if m == NPU - 1 else s_pl, 1)
                    if m == 0 and not first:
                        add_beta(i - 1)
                    if m == 1 and first:
                        norm_rstd(nm, 1, NB - 1)
                    if m == 1 and not first:
                        out_rstd(i - 1)
                    if last and m == 0:
                        norm_rstd(nf, 0, NB)
                if not first:
                    times_gamma(i - 1)

            def add_beta(i):
                xs = x_res[:, bass.ds(i * TPS, TPS), :]
                pool.tensor_tensor(xs, xs, beta_b[:].unsqueeze(1).broadcast_to([P, TPS, D]), ALU.add).then_inc(s_xb, 1)

            def out_rstd(i):
                pool.wait_ge(s_ostat, i + 1)
                pool.tensor_tensor(veps_o[:], mv_o[:, :, 1], eps_c[:], ALU.add).then_inc(s_oveps, 1)
                pool.wait_ge(s_oveps, i + 1)
                pool.tensor_tensor(rstd_o[:], veps_o[:], m_half[:], ALU.pow).then_inc(s_orstd, 1)

            def times_gamma(i):
                pool.wait_ge(s_z, i + 1)
                pool.tensor_tensor(z_mix[:], z_mix[:], gamma_b[:].unsqueeze(1).broadcast_to([P, TPS, D]), ALU.mult).then_inc(s_zg, 1)

            pool.memset(ident[:], 0.0)
            pool.memset(sel_raw[:], 0.0)
            pool.memset(eps_c[:], LN_EPS)
            pool.memset(m_half[:], -0.5).then_inc(s_zero, 1)
            pool.wait_ge(s_zero, 1)
            pool.affine_select(out=ident[:], in_=ident[:], compare_op=ALU.not_equal, fill=1.0,
                               base=0, pattern=[[-1, P]], channel_multiplier=1).then_inc(s_const, 1)
            norm_rstd(nf, 0, 0)
            for k in range(2):
                if k:
                    pool.wait_ge(s_zero, 2)
                t = pool.affine_select(out=sel_raw[:], in_=sel_raw[:], compare_op=ALU.not_equal, fill=1.0,
                                       base=-k * E, pattern=[[-1, E], [0, P]], channel_multiplier=1)
                t.then_inc(s_const if k else s_zero, 1)
            for c in range(0, E, 2):
                if c in (0, 2):
                    pool.wait_ge(s_w1h, 1 + c // 2)
                pool.tensor_tensor(w1_lo[:, c:c + 2, :], w1_raw[:, c:c + 2, :], w1_hi[:, c:c + 2, :].bitcast(F32),
                                   ALU.subtract).then_inc(s_w1l, 1)
            pool.wait_ge(s_w2h, 1)
            for c in range(0, E, 2):
                pool.tensor_tensor(w2_lo[:, c:c + 2, :, :], w2_raw[:, c:c + 2, :, :], w2_hi[:, c:c + 2, :, :].bitcast(F32),
                                   ALU.subtract).then_inc(s_w2l, 1)
            ffn_layer(0)
            pool.wait_ge(s_gb, 32)
            mix_gates(0, True)
            with pool.Fori(1, BATCH - 1) as i:
                mix_gates(i, False)
            mix_gates(BATCH - 1, False, last=True)
            out_rstd(BATCH - 1)
            add_beta(BATCH - 1)
            times_gamma(BATCH - 1)
            ffn_layer(1)


_INS = ['L0_attn_x', 'L0_attn_gate_W', 'L0_attn_value_W', 'L0_attn_gamma', 'L0_attn_beta', 'L0_ffn_router_w', 'L0_ffn_w1', 'L0_ffn_w2']


def kernel(**inputs):
    import numpy as _np
    import concourse.bacc as _bacc
    from concourse import mybir as _mybir
    from concourse.bass_utils import run_bass_kernel_spmd as _run

    nc = _bacc.Bacc("TRN2", target_bir_lowering=False, num_devices=1)
    arrays, args = {}, []
    for name in _INS:
        a = _np.ascontiguousarray(inputs[name])
        arrays[f"in_{name}_dram"] = a
        args.append(nc.dram_tensor(f"in_{name}_dram", a.shape, _mybir.dt.from_np(a.dtype), kind="ExternalInput").ap())
    shape = arrays["in_L0_attn_x_dram"].shape
    args.append(nc.dram_tensor("out_0_dram", shape, _mybir.dt.float32, kind="ExternalOutput").ap())
    macaron_program(nc, *args)
    r = _run(nc, [arrays], core_ids=[0])
    return r.results[0]["out_0_dram"]
```

```python
from contextlib import ExitStack

import concourse.bass as bass
from concourse import mybir

F32 = mybir.dt.float32
F32R = mybir.dt.float32r
ALU = mybir.AluOpType
ACT = mybir.ActivationFunctionType
AX_X = mybir.AxisListType.X

P = 128
SHIFTS = (0, -32, -16, -4, -1, 1, 4, 16, 32)
LN_EPS = 1e-05
BELOW_ALL = -3.0e38


def macaron_program(nc, x_in, gate_W, value_W, gamma, beta, router_w, w1, w2, out):
    BATCH, SEQ, D = x_in.shape
    E, _, FF = w1.shape
    T = BATCH * SEQ
    BLK = 512
    TPB = BLK // P
    NB = T // BLK
    BPS = SEQ // BLK
    FH = FF // P
    NS = len(SHIFTS)
    U = NS + 1
    HALO = max(SHIFTS)
    LAG = 3
    HB = 4
    TPS = SEQ // P
    assert D == P and FH == 2 and BPS == 2 and E % HB == 0 and LAG < HB and E == 8
    MIXW_ROUNDS = (range(0, 4), range(4, 8), range(8, U))
    MIXW_STEPS = (0, 1, 4)
    LATE_TURN, LATE_RSTD, LATE_NORM, LATE_GAMMA, LATE_ADD = (1, 5), (2, 6), (3, 6), (4, 6), (5, 7)
    POOL_UNITS = (2, 5, 8)
    DVE_UNITS = tuple(u for u in range(1, U) if u not in POOL_UNITS)
    NPU, NDU = len(POOL_UNITS), len(DVE_UNITS)

    x_tiles = x_in.rearrange("b s d -> (b s) d").rearrange("(n p) d -> p n d", p=P)
    out_tiles = out.rearrange("b s d -> (b s) d").rearrange("(n p) d -> p n d", p=P)

    def zero(n):
        return isinstance(n, int) and n == 0

    def late(i):
        return isinstance(i, int) and i >= BATCH - 1

    def second_half(i):
        return isinstance(i, int) and i == BATCH

    with ExitStack() as ctx:
        def sb(name, shape, dt=F32):
            return ctx.enter_context(nc.sbuf_tensor(name, shape, dt))

        def psum(name, shape):
            return ctx.enter_context(nc.psum_tensor(name, shape, F32))

        def sem(name):
            return ctx.enter_context(nc.semaphore(name))

        x_res = sb("x_res", [P, NB * TPB, D])
        xT_hi = sb("xT_hi", [P, NB, BLK], F32R)
        xT_lo = sb("xT_lo", [P, NB, BLK], F32R)
        w1_hi = sb("w1_hi", [P, E, FF], F32R)
        w1_lo = sb("w1_lo", [P, E, FF], F32R)
        w2_hi = sb("w2_hi", [P, E, FH, D], F32R)
        w2_lo = sb("w2_lo", [P, E, FH, D], F32R)
        mix_hi = sb("mix_hi", [P, U, P], F32R)
        mix_lo = sb("mix_lo", [P, U, P], F32R)
        rtT = sb("rtT", [P, E])
        xT_full = sb("xT_full", [P, BLK])
        gelu_h = sb("gelu_h", [P, 2, FH, BLK])
        scaled_h = sb("scaled_h", [P, HB, FH, BLK])
        h_hi = sb("h_hi", [P, HB, FH, BLK], F32R)
        h_lo = sb("h_lo", [P, HB, FH, BLK], F32R)
        w_all = sb("w_all", [P, 2, E, BLK])
        v_pad = sb("v_pad", [P, 2, SEQ + 2 * HALO])
        z_mix = sb("z_mix", [P, TPS, D])
        xn_ffn = sb("xn_ffn", [P, TPB, D])
        xn_mix = sb("xn_mix", [P, TPB, D])
        yT = sb("yT", [P, BLK])
        w_copies = sb("w_copies", [P, TPB, P // E, E])
        wT = sb("wT", [P, BLK])
        rt_raw = sb("rt_raw", [E, D])
        ident = sb("ident", [P, P])
        gamma_b = sb("gamma_b", [P, D])
        beta_b = sb("beta_b", [P, D])
        stats = sb("stats", [P, 2, TPB, 6])
        mv = sb("mv", [P, 2, TPB, 2])
        veps = sb("veps", [P, 2, TPB])
        rstd = sb("rstd", [P, 2, TPB])
        stats_o = sb("stats_o", [P, TPS, 6])
        mv_o = sb("mv_o", [P, TPS, 2])
        veps_o = sb("veps_o", [P, TPS])
        rstd_o = sb("rstd_o", [P, TPS])
        nbias_o = sb("nbias_o", [P, TPS])
        m_half = sb("m_half", [P, TPS])
        eps_c = sb("eps_c", [P, TPS])
        wait_pad = sb("wait_pad", [P, 1])
        rank = sb("rank", [P, TPB, E])
        top = sb("top", [P, 8, TPB])
        pick = sb("pick", [P, 5, TPB, E])

        ps_up = psum("ps_up", [P, 2, FH, BLK])
        ps_out = psum("ps_out", [P, 2, BLK])
        ps_t = psum("ps_t", [P, TPB, P])
        ps_r = psum("ps_r", [P, BLK])
        ps_y = ps_out[:, 0, :]
        logits = ps_r[:, :].rearrange("p (t c) -> p t c", c=P)[:, :, 0:E]

        w1_raw = scaled_h[:, 0:2, :, :].rearrange("p a k c -> p (a k c)").rearrange("p (e f) -> p e f", e=E)
        w2_raw = scaled_h[:, 2:4, :, :].rearrange("p a k c -> p (a k c)").rearrange("p (e k d) -> p e k d", e=E, k=FH)
        odd = w_all[:, 1, :, :].rearrange("p e c -> p (e c)")
        pool_mix = odd[:, 0:2 * SEQ].rearrange("p (a c) -> p a c", a=2)
        mixed, acc_d = odd[:, 2 * SEQ:3 * SEQ], odd[:, 3 * SEQ:4 * SEQ]
        mix_raw = pool_mix[:, :, :].rearrange("p a c -> p (a c)")[:, 0:U * D].rearrange("p (u d) -> p u d", u=U)
        prod_d = [gelu_h[:, k, :, :].rearrange("p k c -> p (k c)") for k in range(2)]
        acc_p, prod_p = pool_mix[:, 0, :], pool_mix[:, 1, :]

        s_x0, s_x1, s_w1, s_w2, s_rt, s_mixw, s_gb = (sem(n) for n in ("x0_in", "x1_in", "w1_in", "w2_in", "rt_in", "mixw_in", "gb_in"))
        s_zero, s_const = sem("consts_cleared"), sem("consts_ready")
        s_rank = sem("rank_ready")
        s_rtT, s_rts = sem("router_turned"), sem("router_weights_ready")
        s_w1h, s_w1l, s_w2h, s_w2l = (sem(n) for n in ("w1_hi_ready", "w1_lo_ready", "w2_hi_ready", "w2_lo_ready"))
        s_mixT, s_mixh, s_mixl = sem("mixw_turned"), sem("mixw_hi_ready"), sem("mixw_lo_ready")

        class Norm:
            def __init__(self, n):
                self.link, self.stat, self.veps, self.rstd, self.xn, self.turned, self.split = (
                    sem(f"{n}_{k}") for k in ("link", "stats_ready", "veps_ready", "rstd_ready", "xn_ready", "turned", "split"))
        nf, nm = Norm("ffn"), Norm("mix")
        s_xf, s_lgt = sem("xT_full_ready"), sem("logits_ready")
        s_tl, s_gap, s_tanh, s_wsum, s_wt, s_wT = (sem(n) for n in ("top_link", "gap_ready", "tanh_ready", "weights_ready", "wT_turned", "wT_ready"))
        s_rows = [sem(f"weights_spread_{k}") for k in range(E // 2)]
        s_up, s_gelu, s_scaled, s_hi, s_lo, s_down = (
            sem(n) for n in ("up_done", "gelu_done", "scaled_done", "h_hi_done", "h_lo_done", "down_done"))
        s_lo_last = sem("last_h_lo_done")
        s_yT, s_yt, s_xnew = sem("yT_copied"), sem("y_turned"), sem("x_updated")
        s_mm, s_v, s_gate, s_dg, s_pg, s_dl, s_pl = (
            sem(n) for n in ("mix_product_done", "value_copied", "gate_ready", "dve_gate_used", "pool_gate_used", "dve_mix_link", "pool_mix_link"))
        s_mixed, s_ot, s_ol, s_ostat, s_oveps, s_orstd, s_nb, s_z, s_zg, s_xb = (
            sem(n) for n in ("mixed_ready", "mixed_turned", "out_link", "out_stats_ready", "out_veps_ready",
                             "out_rstd_ready", "out_bias_ready", "z_ready", "z_gamma_ready", "x_beta_ready"))
        s_out = sem("out_stored")

        def part(i):
            if late(i):
                return (i - (BATCH - 1)) * TPB, TPB
            return 0, TPS

        def turned_mix(i, j):
            if late(i):
                return ps_out[:, 1, (j % TPB) * P:(j % TPB + 1) * P]
            return ps_out[:, j // TPB, (j % TPB) * P:(j % TPB + 1) * P]

        def xpart(i):
            first, tiles = part(i)
            if late(i):
                return x_res[:, (BATCH - 1) * TPS + first:(BATCH - 1) * TPS + first + tiles, :]
            return x_res[:, bass.ds(i * TPS, TPS), :]

        def turn_step(first):
            return 2 if first else 1

        def xblk(b):
            return x_res[:, bass.ds(b * TPB, TPB), :]

        block = ctx.enter_context(nc.Block())

        @block.sync
        def _(sp):
            sp.dma_start(x_res[:, 0:TPB, :], x_tiles[:, 0:TPB, :]).then_inc(s_x0, 16)
            sp.dma_start(rt_raw[:], router_w).then_inc(s_rt, 16)
            sp.dma_start(w1_raw, w1.rearrange("e d f -> d e f")).then_inc(s_w1, 16)
            sp.dma_start(w2_raw, w2.rearrange("e (k p) d -> p e k d", p=P)).then_inc(s_w2, 16)
            sp.dma_start(mix_raw[:, 0:1, :], value_W.rearrange("(u e) d -> e u d", e=P)).then_inc(s_mixw, 16)
            sp.dma_start(mix_raw[:, 1:U, :], gate_W.rearrange("(u e) d -> e u d", e=P)).then_inc(s_mixw, 16)
            sp.dma_start(x_res[:, TPB:, :], x_tiles[:, TPB:, :]).then_inc(s_x1, 16)
            sp.dma_start(gamma_b[:], gamma.rearrange("(a d) -> a d", a=1).partition_broadcast(P)).then_inc(s_gb, 16)
            sp.dma_start(beta_b[:], beta.rearrange("(a d) -> a d", a=1).partition_broadcast(P)).then_inc(s_gb, 16)

            def spread_weights(n, par):
                half = w_all[:, bass.ds(par, 1), :, :]
                sp.wait_ge(s_wT, n + 1)
                if isinstance(n, int) and n in (1, NB + 1):
                    sp.wait_ge(s_mixT, len(MIXW_ROUNDS))
                    if n > NB:
                        sp.wait_ge(s_ot, BATCH)
                for k in range(E // 2):
                    for e in (2 * k, 2 * k + 1):
                        rows = wT[e::E, :].unsqueeze(1).broadcast_to([P // E, E, BLK])
                        sp.dma_start(half[:, :, e, :], rows).then_inc(s_rows[k], 16)

            def store(b):
                sp.wait_ge(s_xnew, b + NB + 1)
                sp.dma_start(out_tiles[:, bass.ds(b * TPB, TPB), :], xblk(b)).then_inc(s_out, 16)

            spread_weights(0, 0)
            spread_weights(1, 1)
            with sp.Fori(2, NB) as b:
                spread_weights(b, b % 2)
            spread_weights(NB, 0)
            spread_weights(NB + 1, 1)
            with sp.Fori(2, NB) as b:
                store(b - 2)
                spread_weights(NB + b, b % 2)
            for b in (NB - 2, NB - 1):
                store(b)
            sp.wait_ge(s_out, 16 * NB)

        @block.tensor
        def _(pe):
            def turn_x(s, xn, n, free):
                pe.wait_ge(s.xn, n + 1)
                for sm, v in free:
                    pe.wait_ge(sm, v)
                for j in range(TPB):
                    t = pe.transpose(ps_t[:, j, :], xn[:, j, :], ident[:])
                t.then_inc(s.turned, 1)

            def router(n):
                pe.wait_ge(s_xf, n + 1)
                if not zero(n):
                    pe.wait_ge(s_wT, n)
                for j in range(TPB):
                    t = pe.matmul(ps_r[:, j * P:j * P + E], xT_full[:, j * P:(j + 1) * P], rtT[:], start=True, stop=True)
                t.then_inc(s_lgt, 1)

            def turn_weights(n):
                pe.wait_ge(s_wsum, n + 1)
                for j in range(TPB):
                    t = pe.transpose(ps_r[:, j * P:(j + 1) * P], w_copies[:, j, :, :].rearrange("p r e -> p (r e)"), ident[:])
                t.then_inc(s_wt, 1)

            def up(b, e, g, warm):
                if warm:
                    pe.wait_ge(s_gelu, g - 1)
                for k in range(FH):
                    w = slice(k * P, (k + 1) * P)
                    pe.matmul(ps_up[:, e % 2, k, :], w1_hi[:, e, w], xT_hi[:, bass.ds(b, 1), :], start=True, stop=False)
                    pe.matmul(ps_up[:, e % 2, k, :], w1_hi[:, e, w], xT_lo[:, bass.ds(b, 1), :], start=False, stop=False)
                    t = pe.matmul(ps_up[:, e % 2, k, :], w1_lo[:, e, w], xT_hi[:, bass.ds(b, 1), :], start=False, stop=True)
                t.then_inc(s_up, 1)

            def down(e, g, n):
                pe.wait_ge(s_hi, g + 1)
                if isinstance(g, int) and g == 2 * NB * E - 1:
                    pe.wait_ge(s_lo_last, 1)
                else:
                    pe.wait_ge(s_lo, g + 1)
                if e == 0 and not zero(n):
                    pe.wait_ge(s_yT, n)
                for k in range(FH):
                    pe.matmul(ps_y, w2_hi[:, e, k, :], h_hi[:, e % HB, k, :], start=(e == 0 and k == 0), stop=False)
                    pe.matmul(ps_y, w2_lo[:, e, k, :], h_hi[:, e % HB, k, :], start=False, stop=False)
                    t = pe.matmul(ps_y, w2_hi[:, e, k, :], h_lo[:, e % HB, k, :], start=False, stop=(e == E - 1 and k == FH - 1))
                t.then_inc(s_down, 1)

            def turn_y(n, free):
                pe.wait_ge(s_yT, n + 1)
                for sm, v in free:
                    pe.wait_ge(sm, v)
                for j in range(TPB):
                    t = pe.transpose(ps_t[:, j, :], yT[:, j * P:(j + 1) * P], ident[:])
                t.then_inc(s_yt, 1)

            def ffn_block(layer, b, first, last, second=False):
                n = layer * NB + b
                cold = first and layer == 0
                turn = turn_step(first)
                for e in range(E):
                    g = n * E + e
                    if first and e == 0:
                        pe.wait_ge(nf.split, 2 * n + 2)
                    if cold and e % 2 == 0:
                        pe.wait_ge(s_w1l, e // 2 + 1)
                    if layer == 1 and first and e < 2:
                        pe.wait_ge(s_gate, BATCH * NS - 1 + e)
                    up(b, e, g, not (first and e < 2))
                    if first and e == 0:
                        turn_weights(n)
                    if e == turn + 1 and not last:
                        router(n + 1)
                    if cold and e in MIXW_STEPS:
                        turn_mix_weights(MIXW_STEPS.index(e))
                    if e >= LAG:
                        if cold and (e - LAG) % 2 == 0:
                            pe.wait_ge(s_w2l, (e - LAG) // 2 + 1)
                        down(e - LAG, g - LAG, n)
                    elif not first:
                        down(e - LAG + E, g - LAG, n - 1)
                    if layer == 1 and first and e in LATE_TURN:
                        turn_mixed(BATCH - 1 + LATE_TURN.index(e))
                    if e == turn and not last:
                        if cold:
                            free = [(s_mixl, 2)]
                        elif second and layer == 0:
                            free = [(s_mixl, 3)]
                        elif first:
                            free = []
                        else:
                            free = [(nm.split, 2 * b - 2)] if layer == 0 else [(s_xnew, n - 1)]
                        turn_x(nf, xn_ffn, n + 1, free)
                    if e == 3 and not first:
                        if not last:
                            free = [(nf.split, 2 * n + 4)]
                        else:
                            free = [(nm.split, 2 * b - 2)] if layer == 0 else [(s_xnew, n - 1)]
                        turn_y(n - 1, free)
                    if e == 7 and layer == 0 and not first:
                        turn_x(nm, xn_mix, b - 1, [(s_xnew, b)])
                    if e == 5 and not last:
                        turn_weights(n + 1)

            def ffn_layer(layer):
                ffn_block(layer, 0, True, False)
                if layer == 0:
                    ffn_block(layer, 1, False, False, second=True)
                with pe.Fori(2 - layer, NB - 1) as b:
                    ffn_block(layer, b, False, False)
                ffn_block(layer, NB - 1, False, True)
                n = layer * NB + NB - 1
                for e in range(E - LAG, E):
                    down(e, n * E + e, n)
                    if layer == 0 and e < E - 1:
                        mix_unit(0, e - (E - LAG), True)
                if layer == 1:
                    turn_y(n, [(s_xnew, n)])

            def turn_mix_weights(r):
                if r == 0:
                    pe.wait_ge(s_mixw, 32)
                elif r == 1:
                    pe.wait_ge(s_mixl, 1)
                else:
                    pe.wait_ge(nf.split, 4)
                for k, u in enumerate(MIXW_ROUNDS[r]):
                    t = pe.transpose(ps_t[:, k, :], mix_raw[:, u, :], ident[:])
                t.then_inc(s_mixT, 1)

            def turn_mixed(i):
                t0, tiles = part(i)
                if second_half(i):
                    pe.wait_ge(s_z, i)
                else:
                    pe.wait_ge(s_mixed, i + 1)
                for j in range(t0, t0 + tiles):
                    t = pe.transpose(turned_mix(i, j), mixed[:, j * P:(j + 1) * P], ident[:])
                t.then_inc(s_ot, 1)

            def mix_unit(i, u, first):
                if first and u < 2:
                    pe.wait_ge(s_gelu, NB * E - 1 + u)
                elif u == 0:
                    pe.wait_ge(s_gate, i * NS - 1)
                elif u == 1:
                    pe.wait_ge(s_gate, i * NS)
                elif u == 2:
                    pe.wait_ge(s_v, i + 1)
                else:
                    pe.wait_ge(s_gate, i * NS + u - 2)
                for k in range(BPS):
                    if u == 0:
                        pe.wait_ge(nm.split, 4 * i + 2 * k + 2)
                    xb = bass.ds(i * BPS + k, 1)
                    pe.matmul(ps_up[:, u % 2, k, :], mix_hi[:, u, :], xT_hi[:, xb, :], start=True, stop=False)
                    pe.matmul(ps_up[:, u % 2, k, :], mix_hi[:, u, :], xT_lo[:, xb, :], start=False, stop=False)
                    t = pe.matmul(ps_up[:, u % 2, k, :], mix_lo[:, u, :], xT_hi[:, xb, :], start=False, stop=True)
                t.then_inc(s_mm, 1)

            def mix_seq(i, first, last=False):
                for u in range(2 if first else 0, U):
                    if first and u == 3:
                        turn_y(NB - 1, [(nm.split, 2 * NB - 2)])
                    if last and u == 9:
                        turn_x(nf, xn_ffn, NB, [])
                    mix_unit(i, u, first)
                    if u == 4 and not first:
                        turn_mixed(i - 1)
                if first:
                    turn_x(nm, xn_mix, NB - 1, [(s_xnew, NB)])
                if last:
                    router(NB)

            pe.wait_ge(s_const, 1)
            pe.wait_ge(s_rt, 16)
            pe.transpose(ps_t[:, 0, 0:E], rt_raw[:], ident[0:E, 0:E]).then_inc(s_rtT, 1)
            turn_x(nf, xn_ffn, 0, [(s_rts, 1)])
            router(0)
            ffn_layer(0)
            mix_seq(0, True)
            with pe.Fori(1, BATCH - 1) as i:
                mix_seq(i, False)
            mix_seq(BATCH - 1, False, last=True)
            ffn_layer(1)

        @block.scalar
        def _(act):
            def gap_tanh(n):
                act.wait_ge(s_gap, n + 1)
                act.activation(top[:, 5, :], top[:, 4, :], ACT.Tanh, scale=0.5).then_inc(s_tanh, 1)

            def norm_round(s, b, n):
                act.wait_ge(s.turned, n + 1)
                if s is nf:
                    if not zero(n):
                        act.wait_ge(s_lgt, n)
                    act.activation(xT_full[:], ps_t[:].rearrange("p t c -> p (t c)"), ACT.Copy).then_inc(s_xf, 1)
                act.activation(xT_hi[:, bass.ds(b, 1), :], ps_t[:], ACT.Copy).then_inc(s.split, 1)

            def weights_copy(n):
                act.wait_ge(s_wt, n + 1)
                if not zero(n):
                    for rows in s_rows:
                        act.wait_ge(rows, 32 * n)
                act.activation(wT[:], ps_r[:], ACT.Copy).then_inc(s_wT, 1)

            def gelu(e, g, warm):
                act.wait_ge(s_up, g + 1)
                if warm:
                    act.wait_ge(s_scaled, g - 1)
                act.activation(gelu_h[:, e % 2, :, :], ps_up[:, e % 2, :, :], ACT.Gelu).then_inc(s_gelu, 1)

            def h_round(e, g, warm):
                act.wait_ge(s_scaled, g + 1)
                if warm:
                    act.wait_ge(s_down, g - HB + 1)
                act.activation(h_hi[:, e % HB, :, :], scaled_h[:, e % HB, :, :], ACT.Copy).then_inc(s_hi, 1)

            def y_copy(n):
                act.wait_ge(s_down, (n + 1) * E)
                act.activation(yT[:], ps_y, ACT.Copy).then_inc(s_yT, 1)

            def ffn_block(layer, b, first, last):
                n = layer * NB + b
                cold = first and layer == 0
                for e in range(E):
                    g = n * E + e
                    if e == 6 and not last:
                        weights_copy(n + 1)
                    if e == turn_step(first) + 1 and not last:
                        norm_round(nf, b + 1, n + 1)
                    if e == LAG and not first:
                        y_copy(n - 1)
                    if cold and e - 1 in MIXW_STEPS:
                        mix_weights_round(MIXW_STEPS.index(e - 1))
                    if layer == 1 and first and e < 2:
                        act.wait_ge(s_dl, BATCH * (NDU - 1) - 1 + e)
                    gelu(e, g, not (first and e < 2))
                    if first and e == 0:
                        weights_copy(n)
                    if e >= 1:
                        h_round(e - 1, g - 1, not (cold and e - 1 < HB))
                        if layer == 1 and first and e in LATE_NORM:
                            normalise_out(BATCH - 1 + LATE_NORM.index(e))
                    elif not first:
                        h_round(E - 1, g - 1, True)
                    if e == turn_step(first) + 2 and not last:
                        gap_tanh(n + 1)
                    if e == 7 and layer == 0 and not first:
                        norm_round(nm, b - 1, b - 1)

            def ffn_layer(layer):
                ffn_block(layer, 0, True, False)
                with act.Fori(1, NB - 1) as b:
                    ffn_block(layer, b, False, False)
                ffn_block(layer, NB - 1, False, True)
                n = layer * NB + NB - 1
                h_round(E - 1, n * E + E - 1, True)
                if layer == 1:
                    y_copy(n)

            def mix_weights_round(r):
                us = MIXW_ROUNDS[r]
                act.wait_ge(s_mixT, r + 1)
                act.activation(mix_hi[:, us[0]:us[-1] + 1, :], ps_t[:, 0:len(us), :], ACT.Copy).then_inc(s_mixh, 1)

            def normalise_out(i):
                act.wait_ge(s_nb, i + 1)
                act.wait_ge(s_ot, i + 1)
                t0, tiles = part(i)
                for j in range(t0, t0 + tiles):
                    t = act.activation(z_mix[:, j, :], turned_mix(i, j), ACT.Identity,
                                       bias=nbias_o[:, j:j + 1], scale=rstd_o[:, j:j + 1])
                t.then_inc(s_z, 1)

            def gate(i, u, first):
                act.wait_ge(s_mm, i * U + u + 1)
                prev, turn = (u - HB, 0) if u > HB else (u + (NS - u) // HB * HB, 1)
                if first and turn:
                    act.wait_ge(s_lo, NB * E - HB + u)
                else:
                    if prev in POOL_UNITS:
                        act.wait_ge(s_pg, (i - turn) * NPU + POOL_UNITS.index(prev) + 1)
                    else:
                        act.wait_ge(s_dg, (i - turn) * NDU + DVE_UNITS.index(prev) + 1)
                act.activation(scaled_h[:, (u - 1) % HB, :, :], ps_up[:, u % 2, :, :], ACT.Sigmoid).then_inc(s_gate, 1)

            def value_copy(i):
                act.wait_ge(s_mm, i * U + 1)
                v = v_pad[:, bass.ds(i % 2, 1), :].rearrange("p a c -> p (a c)")
                pv = ps_up[:, 0, :, :].rearrange("p k c -> p (k c)")
                act.activation(v[:, HALO:HALO + SEQ], pv, ACT.Copy)
                act.activation(v[:, 0:HALO], pv[:, SEQ - HALO:SEQ], ACT.Copy)
                act.activation(v[:, HALO + SEQ:], pv[:, 0:HALO], ACT.Copy).then_inc(s_v, 1)

            def mix_seq(i, first, last=False):
                value_copy(i)
                for u in range(1, U):
                    gate(i, u, first)
                    if first and u == 1:
                        y_copy(NB - 1)
                    if not first and u == 8:
                        normalise_out(i - 1)
                    if last and u == 8:
                        norm_round(nf, 0, NB)
                if first:
                    norm_round(nm, NB - 1, NB - 1)
                if last:
                    gap_tanh(NB)

            act.wait_ge(s_w1, 16)
            act.activation(w1_hi[:, 0:2, :], w1_raw[:, 0:2, :], ACT.Copy).then_inc(s_w1h, 1)
            act.activation(w1_hi[:, 2:E, :], w1_raw[:, 2:E, :], ACT.Copy).then_inc(s_w1h, 1)
            norm_round(nf, 0, 0)
            act.wait_ge(s_w2, 16)
            act.activation(w2_hi[:], w2_raw, ACT.Copy).then_inc(s_w2h, 1)
            gap_tanh(0)
            ffn_layer(0)
            mix_seq(0, True)
            with act.Fori(1, BATCH - 1) as i:
                mix_seq(i, False)
            mix_seq(BATCH - 1, False, last=True)
            ffn_layer(1)

        @block.vector
        def _(dve):
            def norm_stats(s, w, xb, n):
                for j in range(TPB):
                    t = dve.bn_stats(stats[:, w, j, :], xb(j))
                t.then_inc(s.link, 1)
                dve.wait_ge(s.link, n + 1)
                dve.memset(wait_pad[:], 0.0)
                for j in range(TPB):
                    t = dve.bn_aggr(mv[:, w, j, :], stats[:, w, j, :])
                t.then_inc(s.stat, 1)

            def norm_apply(s, w, xb, xn, n):
                dve.wait_ge(s.rstd, n + 1)
                for j in range(TPB):
                    t = dve.tensor_scalar(xn[:, j, :], xb(j), mv[:, w, j, 0:1], rstd[:, w, j:j + 1], ALU.subtract, ALU.mult)
                t.then_inc(s.xn, 1)

            def norm_split(s, b, n):
                dve.wait_ge(s.split, 2 * n + 1)
                src = ps_t[:, :, :].rearrange("p j c -> p (j c)")
                hi = xT_hi[:, bass.ds(b, 1), :].rearrange("p a c -> p (a c)")
                lo = xT_lo[:, bass.ds(b, 1), :].rearrange("p a c -> p (a c)")
                dve.tensor_tensor(lo, src, hi.bitcast(F32), ALU.subtract).then_inc(s.split, 1)

            TOP_LINKS = 15

            def link(t, n, k):
                t.then_inc(s_tl, 1)
                dve.wait_ge(s_tl, TOP_LINKS * n + k)

            def spread_e(ap):
                return ap.unsqueeze(2).broadcast_to([P, TPB, E])

            def best(n):
                v1, r1, v2, r2, gap = (top[:, k, :] for k in range(5))
                k1, s1, lg2, k2, s2 = (pick[:, k, :, :] for k in range(5))
                dve.wait_ge(s_lgt, n + 1)
                link(dve.tensor_reduce(v1, logits, AX_X, ALU.max), n, 1)
                link(dve.tensor_tensor(k1, logits, spread_e(v1), ALU.is_equal), n, 2)
                link(dve.tensor_tensor(k1, k1, rank[:], ALU.mult), n, 3)
                link(dve.tensor_reduce(r1, k1, AX_X, ALU.max), n, 4)
                link(dve.tensor_tensor(s1, k1, spread_e(r1), ALU.is_equal), n, 5)
                link(dve.scalar_tensor_tensor(lg2, s1, BELOW_ALL, logits, ALU.mult, ALU.add), n, 6)

            def second_best(n):
                v1, r1, v2, r2, gap = (top[:, k, :] for k in range(5))
                k1, s1, lg2, k2, s2 = (pick[:, k, :, :] for k in range(5))
                link(dve.tensor_reduce(v2, lg2, AX_X, ALU.max), n, 7)
                dve.tensor_tensor(gap, v1, v2, ALU.subtract).then_inc(s_gap, 1)
                link(dve.tensor_tensor(k2, lg2, spread_e(v2), ALU.is_equal), n, 8)
                link(dve.tensor_tensor(k2, k2, rank[:], ALU.mult), n, 9)
                link(dve.tensor_reduce(r2, k2, AX_X, ALU.max), n, 10)
                link(dve.tensor_tensor(s2, k2, spread_e(r2), ALU.is_equal), n, 11)

            def expert_weights(n):
                th, wa, wb = (top[:, k, :] for k in (5, 6, 7))
                s1, s2 = pick[:, 1, :, :], pick[:, 4, :, :]
                dve.wait_ge(s_tanh, n + 1)
                link(dve.tensor_scalar(wa, th, 0.25, 0.25, ALU.mult, ALU.add), n, 12)
                link(dve.tensor_scalar(wb, th, -0.25, 0.25, ALU.mult, ALU.add), n, 13)
                link(dve.tensor_tensor(s1, s1, spread_e(wa), ALU.mult), n, 14)
                link(dve.tensor_tensor(s2, s2, spread_e(wb), ALU.mult), n, 15)
                c1, c2 = (s.unsqueeze(2).broadcast_to([P, TPB, P // E, E]) for s in (s1, s2))
                dve.tensor_tensor(w_copies[:], c1, c2, ALU.add).then_inc(s_wsum, 1)

            def mix_weights_rest(r):
                us = MIXW_ROUNDS[r]
                w = slice(us[0], us[-1] + 1)
                dve.wait_ge(s_mixh, r + 1)
                dve.tensor_tensor(mix_lo[:, w, :], ps_t[:, 0:len(us), :], mix_hi[:, w, :].bitcast(F32), ALU.subtract).then_inc(s_mixl, 1)

            def scale_h(e, g, n, par, warm):
                dve.wait_ge(s_gelu, g + 1)
                if e % 2 == 0:
                    dve.wait_ge(s_rows[e // 2], 32 * (n + 1))
                if warm:
                    dve.wait_ge(s_lo, g - HB + 1)
                w = w_all[:, bass.ds(par, 1), e, :].broadcast_to([P, FH, BLK])
                dve.tensor_tensor(scaled_h[:, e % HB, :, :], gelu_h[:, e % 2, :, :], w, ALU.mult).then_inc(s_scaled, 1)

            def last_h_rest():
                g = 2 * NB * E - 1
                dve.wait_ge(s_hi, g + 1)
                dve.wait_ge(s_down, g - HB + 1)
                dve.tensor_tensor(h_lo[:, g % HB, :, :], scaled_h[:, g % HB, :, :], h_hi[:, g % HB, :, :].bitcast(F32),
                                  ALU.subtract).then_inc(s_lo_last, 1)

            def residual(b, n):
                dve.wait_ge(s_yt, n + 1)
                dve.tensor_tensor(xblk(b), ps_t[:], xblk(b), ALU.add).then_inc(s_xnew, 1)

            def xtile(b):
                return lambda j: x_res[:, bass.ds(b * TPB + j, 1), :].rearrange("p a d -> p (a d)")

            def ffn_block(layer, b, first, last):
                n = layer * NB + b
                cold = first and layer == 0
                for e in range(E):
                    g = n * E + e
                    if cold and e == 0:
                        dve.wait_ge(s_w1l, E // 2)
                    if cold and e == 2:
                        dve.wait_ge(s_w2l, E // 2)
                    if e == 0 and not last:
                        if cold:
                            dve.wait_ge(s_x1, 16)
                        norm_stats(nf, 0, xtile(b + 1), n + 1)
                    if e == 1 and not last:
                        norm_apply(nf, 0, xtile(b + 1), xn_ffn, n + 1)
                    scale_h(e, g, n, b % 2, not (cold and e < HB))
                    if layer == 1 and first and e in LATE_TURN:
                        mix_stats(BATCH - 1 + LATE_TURN.index(e))
                    if layer == 1 and first and e in LATE_RSTD:
                        mix_bias(BATCH - 1 + LATE_RSTD.index(e))
                    if e == turn_step(first) + 1 and not last:
                        norm_split(nf, b + 1, n + 1)
                        best(n + 1)
                    if layer == 0 and not first:
                        if e == 5:
                            dve.wait_ge(s_xnew, n)
                            dve.memset(wait_pad[:], 0.0)
                            norm_stats(nm, 1, xtile(b - 1), b - 1)
                        if e == 6:
                            norm_apply(nm, 1, xtile(b - 1), xn_mix, b - 1)
                        if e == 7:
                            norm_split(nm, b - 1, b - 1)
                    if e == turn_step(first) + 2 and not last:
                        second_best(n + 1)
                    if e == 4 and not last:
                        expert_weights(n + 1)
                    if e == 4 and not first:
                        residual(b - 1, n - 1)
                    if cold and e in MIXW_STEPS:
                        mix_weights_rest(MIXW_STEPS.index(e))
                    if layer == 1 and first and e in LATE_ADD:
                        mix_residual(BATCH - 1 + LATE_ADD.index(e))

            def ffn_layer(layer):
                ffn_block(layer, 0, True, False)
                with dve.Fori(1, NB - 1) as b:
                    ffn_block(layer, b, False, False)
                ffn_block(layer, NB - 1, False, True)
                n = layer * NB + NB - 1
                if layer == 1:
                    last_h_rest()
                    residual(NB - 1, n)

            def gated(i, m, first):
                u = DVE_UNITS[m]
                if m == 0 and not first:
                    dve.wait_ge(s_mixed, i)
                if m > 2:
                    dve.wait_ge(s_dl, i * (NDU - 1) + m - 2)
                dve.wait_ge(s_gate, i * NS + u)
                v = v_pad[:, bass.ds(i % 2, 1), :].rearrange("p a c -> p (a c)")
                g = scaled_h[:, (u - 1) % HB, :, :].rearrange("p k c -> p (k c)")
                vs = v[:, HALO + SHIFTS[u - 1]:HALO + SHIFTS[u - 1] + SEQ]
                dve.tensor_tensor(prod_d[m % 2] if m else acc_d, g, vs, ALU.mult).then_inc(s_dg, 1)

            def add_gated(i, m):
                dve.wait_ge(s_dg, i * NDU + m + 1)
                if m > 1:
                    dve.wait_ge(s_dl, i * (NDU - 1) + m - 1)
                dve.tensor_tensor(acc_d, acc_d, prod_d[m % 2], ALU.add).then_inc(s_dl, 1)

            def mix_gates(i, first, last=False):
                dve.wait_ge(s_v, i + 1)
                gated(i, 0, first)
                if first:
                    residual(NB - 1, NB - 1)
                else:
                    mix_stats(i - 1)
                if last:
                    norm_stats(nf, 0, xtile(0), NB)
                gated(i, 1, first)
                if first:
                    dve.wait_ge(s_xnew, NB)
                    norm_stats(nm, 1, xtile(NB - 1), NB - 1)
                for m in range(2, NDU):
                    if m == 5 and last:
                        norm_split(nf, 0, NB)
                        best(NB)
                        second_best(NB)
                    gated(i, m, first)
                    add_gated(i, m - 1)
                    if m == 2 and last:
                        norm_apply(nf, 0, xtile(0), xn_ffn, NB)
                    if m == 2 and not first:
                        mix_bias(i - 1)
                    if m == 3 and first:
                        norm_apply(nm, 1, xtile(NB - 1), xn_mix, NB - 1)
                if last:
                    expert_weights(NB)
                add_gated(i, NDU - 1)
                if first:
                    norm_split(nm, NB - 1, NB - 1)
                dve.wait_ge(s_dl, (i + 1) * (NDU - 1))
                dve.wait_ge(s_pl, (i + 1) * (NPU - 1))
                if not first:
                    dve.wait_ge(s_ot, i)
                dve.tensor_tensor(mixed, acc_d, acc_p, ALU.add).then_inc(s_mixed, 1)
                if not first:
                    mix_residual(i - 1)

            def mix_stats(i):
                t0, tiles = part(i)
                dve.wait_ge(s_ot, i + 1)
                for j in range(t0, t0 + tiles):
                    t = dve.bn_stats(stats_o[:, j, :], turned_mix(i, j))
                t.then_inc(s_ol, 1)
                dve.wait_ge(s_ol, i + 1)
                dve.memset(wait_pad[:], 0.0)
                for j in range(t0, t0 + tiles):
                    t = dve.bn_aggr(mv_o[:, j, :], stats_o[:, j, :])
                t.then_inc(s_ostat, 1)

            def mix_bias(i):
                dve.wait_ge(s_orstd, i + 1)
                w = slice(part(i)[0], sum(part(i)))
                dve.scalar_tensor_tensor(nbias_o[:, w], mv_o[:, w, 0], -1.0, rstd_o[:, w], ALU.mult, ALU.mult).then_inc(s_nb, 1)

            def mix_residual(i):
                dve.wait_ge(s_zg, i + 1)
                if not second_half(i):
                    dve.wait_ge(s_xb, i + 1)
                dve.tensor_tensor(xpart(i), xpart(i), z_mix[:, part(i)[0]:sum(part(i)), :], ALU.add)

            for e in range(E):
                t = dve.memset(rank[:, :, e:e + 1], float(E - e))
            t.then_inc(s_rank, 1)
            dve.wait_ge(s_x0, 16)
            norm_stats(nf, 0, lambda j: x_res[:, j, :], 0)
            dve.wait_ge(s_rtT, 1)
            dve.tensor_copy(rtT[:], ps_t[:, 0, 0:E]).then_inc(s_rts, 1)
            norm_apply(nf, 0, lambda j: x_res[:, j, :], xn_ffn, 0)
            norm_split(nf, 0, 0)
            dve.wait_ge(s_rank, 1)
            best(0)
            second_best(0)
            expert_weights(0)
            ffn_layer(0)
            mix_gates(0, True)
            with dve.Fori(1, BATCH - 1) as i:
                mix_gates(i, False)
            mix_gates(BATCH - 1, False, last=True)
            ffn_layer(1)

        @block.gpsimd
        def _(pool):
            def norm_rstd(s, w, n):
                pool.wait_ge(s.stat, n + 1)
                pool.tensor_tensor(veps[:, w, :], mv[:, w, :, 1], eps_c[:, 0:TPB], ALU.add).then_inc(s.veps, 1)
                pool.wait_ge(s.veps, n + 1)
                pool.tensor_tensor(rstd[:, w, :], veps[:, w, :], m_half[:, 0:TPB], ALU.pow).then_inc(s.rstd, 1)

            def h_rest(e, g, warm):
                pool.wait_ge(s_hi, g + 1)
                if warm:
                    pool.wait_ge(s_down, g - HB + 1)
                pool.tensor_tensor(h_lo[:, e % HB, :, :], scaled_h[:, e % HB, :, :], h_hi[:, e % HB, :, :].bitcast(F32),
                                   ALU.subtract).then_inc(s_lo, 1)

            def ffn_block(layer, b, first, last):
                n = layer * NB + b
                cold = first and layer == 0
                for e in range(E):
                    g = n * E + e
                    if layer == 1 and first and e in LATE_RSTD:
                        out_rstd(BATCH - 1 + LATE_RSTD.index(e))
                    if e == 0 and not last:
                        norm_rstd(nf, 0, n + 1)
                    if e == 6 and layer == 0 and not first:
                        norm_rstd(nm, 1, b - 1)
                    if e >= 1:
                        h_rest(e - 1, g - 1, not (cold and e - 1 < HB))
                    elif not first:
                        h_rest(E - 1, g - 1, True)
                    if layer == 1 and first and e in LATE_GAMMA:
                        times_gamma(BATCH - 1 + LATE_GAMMA.index(e))

            def ffn_layer(layer):
                ffn_block(layer, 0, True, False)
                with pool.Fori(1, NB - 1) as b:
                    ffn_block(layer, b, False, False)
                ffn_block(layer, NB - 1, False, True)
                if layer == 0:
                    h_rest(E - 1, NB * E - 1, True)

            def mix_gates(i, first, last=False):
                v = v_pad[:, bass.ds(i % 2, 1), :].rearrange("p a c -> p (a c)")
                pool.wait_ge(s_v, i + 1)
                for m, u in enumerate(POOL_UNITS):
                    if m == NPU - 1 and not first:
                        times_gamma(i - 1)
                    pool.wait_ge(s_gate, i * NS + u)
                    if m == 1 and not first:
                        pool.wait_ge(s_mixed, i)
                    if m != 1 and not (first and m == 0):
                        pool.wait_ge(s_pl, i * (NPU - 1) + m // 2)
                    g = scaled_h[:, (u - 1) % HB, :, :].rearrange("p k c -> p (k c)")
                    vs = v[:, HALO + SHIFTS[u - 1]:HALO + SHIFTS[u - 1] + SEQ]
                    pool.tensor_tensor(acc_p if m == 1 else prod_p, g, vs, ALU.mult).then_inc(s_pg, 1)
                    if m == 0 and not first:
                        add_beta(i - 1)
                        out_rstd(i - 1)
                    if m == 0 and last:
                        norm_rstd(nf, 0, NB)
                    if m == 1 and first:
                        norm_rstd(nm, 1, NB - 1)
                    if m == NPU - 1 and last:
                        add_beta(i)
                    if m > 0:
                        pool.wait_ge(s_pg, i * NPU + m + 1)
                        pool.tensor_tensor(acc_p, acc_p, prod_p, ALU.add).then_inc(s_pl, 1)

            def add_beta(i):
                xs = x_res[:, bass.ds(i * TPS, TPS), :]
                pool.tensor_tensor(xs, xs, beta_b[:].unsqueeze(1).broadcast_to([P, TPS, D]), ALU.add).then_inc(s_xb, 1)

            def out_rstd(i):
                pool.wait_ge(s_ostat, i + 1)
                w = slice(part(i)[0], sum(part(i)))
                pool.tensor_tensor(veps_o[:, w], mv_o[:, w, 1], eps_c[:, w], ALU.add).then_inc(s_oveps, 1)
                pool.wait_ge(s_oveps, i + 1)
                pool.tensor_tensor(rstd_o[:, w], veps_o[:, w], m_half[:, w], ALU.pow).then_inc(s_orstd, 1)

            def times_gamma(i):
                pool.wait_ge(s_z, i + 1)
                z = z_mix[:, part(i)[0]:sum(part(i)), :]
                pool.tensor_tensor(z, z, gamma_b[:].unsqueeze(1).broadcast_to([P, part(i)[1], D]), ALU.mult).then_inc(s_zg, 1)

            pool.memset(ident[:], 0.0)
            pool.memset(eps_c[:], LN_EPS)
            pool.memset(m_half[:], -0.5).then_inc(s_zero, 1)
            pool.wait_ge(s_zero, 1)
            pool.affine_select(out=ident[:], in_=ident[:], compare_op=ALU.not_equal, fill=1.0,
                               base=0, pattern=[[-1, P]], channel_multiplier=1).then_inc(s_const, 1)
            norm_rstd(nf, 0, 0)
            for c in range(0, E, 2):
                if c in (0, 2):
                    pool.wait_ge(s_w1h, 1 + c // 2)
                pool.tensor_tensor(w1_lo[:, c:c + 2, :], w1_raw[:, c:c + 2, :], w1_hi[:, c:c + 2, :].bitcast(F32),
                                   ALU.subtract).then_inc(s_w1l, 1)
            pool.wait_ge(s_w2h, 1)
            for c in range(0, E, 2):
                pool.tensor_tensor(w2_lo[:, c:c + 2, :, :], w2_raw[:, c:c + 2, :, :], w2_hi[:, c:c + 2, :, :].bitcast(F32),
                                   ALU.subtract).then_inc(s_w2l, 1)
            ffn_layer(0)
            pool.wait_ge(s_gb, 32)
            mix_gates(0, True)
            with pool.Fori(1, BATCH - 1) as i:
                mix_gates(i, False)
            mix_gates(BATCH - 1, False, last=True)
            ffn_layer(1)


_INS = ['L0_attn_x', 'L0_attn_gate_W', 'L0_attn_value_W', 'L0_attn_gamma', 'L0_attn_beta', 'L0_ffn_router_w', 'L0_ffn_w1', 'L0_ffn_w2']


def kernel(**inputs):
    import numpy as _np
    import concourse.bacc as _bacc
    from concourse import mybir as _mybir
    from concourse.bass_utils import run_bass_kernel_spmd as _run

    nc = _bacc.Bacc("TRN2", target_bir_lowering=False, num_devices=1)
    arrays, args = {}, []
    for name in _INS:
        a = _np.ascontiguousarray(inputs[name])
        arrays[f"in_{name}_dram"] = a
        args.append(nc.dram_tensor(f"in_{name}_dram", a.shape, _mybir.dt.from_np(a.dtype), kind="ExternalInput").ap())
    shape = arrays["in_L0_attn_x_dram"].shape
    args.append(nc.dram_tensor("out_0_dram", shape, _mybir.dt.float32, kind="ExternalOutput").ap())
    macaron_program(nc, *args)
    r = _run(nc, [arrays], core_ids=[0])
    return r.results[0]["out_0_dram"]
```
